# Optimizing a Trainium2 kernel written in Bass

```python
import numpy as np
import jax
import jax.numpy as jnp

def _softmax(x, axis=-1):
    return jax.nn.softmax(x, axis=axis)

def _gelu(x):
    return jax.nn.gelu(x, approximate=True)

def _silu(x):
    return jax.nn.silu(x)

def _sigmoid(x):
    return jax.nn.sigmoid(x)

def _layernorm(x, axis=-1, eps=1e-05):
    m = jnp.mean(x, axis=axis, keepdims=True)
    v = jnp.var(x, axis=axis, keepdims=True)
    return (x - m) / jnp.sqrt(v + eps)

def _scatter_add(tgt, idx, src, axis=0):
    return tgt.at[idx].add(src)

def _segment_sum(src, seg, n):
    return jax.ops.segment_sum(src, seg, n)
kernel_name = 'mk_conv_attn_hybrid_d2_conv_nchw128_r2_8d187c'

def setup_inputs(seed: int=0):
    np.random.seed(seed)
    _w = jnp.asarray

    def _rec_inputs():
        import jax
        import jax.numpy as jnp
        _gk = jax.random.key(seed)
        x = -0.0005207 + 1.001 * jax.random.normal(jax.random.fold_in(_gk, 1), (4, 64, 32, 32), jnp.float32)
        return x
    x = _rec_inputs()

    def _L0_conv_setup():
        import jax, jax.numpy as jnp
        import numpy as np
        D_CONV = 4
        D_STATE = 16
        GROUP = 8

        def _ln(x, g, b):
            mu = x.mean(-1, keepdims=True)
            v = ((x - mu) ** 2).mean(-1, keepdims=True)
            return (x - mu) * jax.lax.rsqrt(v + 1e-05) * g + b

        def _mamba(x, W_in, conv_w, conv_b, W_x, W_dt, b_dt, A_log, D_skip, W_out):
            B, L, Dm = x.shape
            d_inner = W_in.shape[0] // 2
            dt_rank = W_dt.shape[1]
            xz = x @ W_in.T
            xi, z = (xz[..., :d_inner], xz[..., d_inner:])
            xc = jax.lax.conv_general_dilated(xi.transpose(0, 2, 1), conv_w, (1,), [(D_CONV - 1, 0)], feature_group_count=d_inner, dimension_numbers=('NCH', 'OIH', 'NCH'))
            u = jax.nn.silu((xc + conv_b[:, None]).transpose(0, 2, 1))
            x_dbl = u @ W_x.T
            dt = jax.nn.softplus(x_dbl[..., :dt_rank] @ W_dt.T + b_dt)
            Bs = x_dbl[..., dt_rank:dt_rank + D_STATE]
            Cs = x_dbl[..., dt_rank + D_STATE:]
            A = -jnp.exp(A_log)

            def step(h, inp):
                dt_t, B_t, C_t, u_t = inp
                dA = jnp.exp(dt_t[..., None] * A)
                h = dA * h + (dt_t * u_t)[..., None] * B_t[:, None, :]
                return (h, jnp.einsum('bdn,bn->bd', h, C_t))
            h0 = jnp.zeros((B, d_inner, D_STATE), x.dtype)
            _, ys = jax.lax.scan(step, h0, (dt.transpose(1, 0, 2), Bs.transpose(1, 0, 2), Cs.transpose(1, 0, 2), u.transpose(1, 0, 2)))
            y = ys.transpose(1, 0, 2) + u * D_skip
            return y * jax.nn.silu(z) @ W_out.T
        key = jax.random.key(seed)
        ks = jax.random.split(key, 10)
        B, C, W, H = (4, 64, 32, 32)
        out_dim = 64
        d_inner = 2 * C
        dt_rank = (C + 15) // 16
        f = lambda k, s, sc=0.02: jax.random.normal(k, s, jnp.float32) * sc
        A_log = jnp.log(jnp.tile(jnp.arange(1, D_STATE + 1, dtype=jnp.float32), (d_inner, 1)))
        return dict(x=jax.random.normal(ks[0], (B, C, W, H), jnp.float32), gamma=jnp.ones((C,), jnp.float32), beta=jnp.zeros((C,), jnp.float32), W_in=f(ks[1], (2 * d_inner, C)), conv_w=f(ks[2], (d_inner, 1, D_CONV), 0.1), conv_b=jnp.zeros((d_inner,), jnp.float32), W_x=f(ks[3], (dt_rank + 2 * D_STATE, d_inner)), W_dt=f(ks[4], (d_inner, dt_rank), 0.1), b_dt=f(ks[5], (d_inner,), 0.5), A_log=A_log, D_skip=jnp.ones((d_inner,), jnp.float32), W_out=f(ks[6], (C, d_inner)), W_p=f(ks[7], (out_dim, C)), b_p=jnp.zeros((out_dim,), jnp.float32), s1=jnp.ones((1,), jnp.float32), s2=jnp.ones((1,), jnp.float32))
    _L0_conv_all = _L0_conv_setup()
    _L0_conv_in = {k: v for k, v in _L0_conv_all.items() if k in ('gamma', 'beta', 'W_in', 'conv_w', 'conv_b', 'W_x', 'W_dt', 'b_dt', 'A_log', 'D_skip', 'W_out', 'W_p', 'b_p', 's1', 's2')}
    del _L0_conv_all

    def _L1_attn_setup():
        import jax, jax.numpy as jnp
        import numpy as np
        B, T, C = (4, 2048, 64)
        key = jax.random.key(seed)
        k1, k2, k3, k4 = jax.random.split(key, 4)
        x = jax.random.normal(k1, (B, T, C), dtype=jnp.float32)
        s = 1.0 / np.sqrt(C)
        Wq = jax.random.normal(k2, (C, C), dtype=jnp.float32) * s
        Wk = jax.random.normal(k3, (C, C), dtype=jnp.float32) * s
        Wv = jax.random.normal(k4, (C, C), dtype=jnp.float32) * s
        return {'x': x, 'Wq': Wq, 'Wk': Wk, 'Wv': Wv}
    _L1_attn_all = _L1_attn_setup()
    _L1_attn_in = {k: v for k, v in _L1_attn_all.items() if k in ('Wq', 'Wk', 'Wv')}
    del _L1_attn_all

    def _L1_ffn_setup():
        import jax, jax.numpy as jnp
        import numpy as np
        NB, NOPS = (33, 19)
        D, H = (64, 256)
        B, S = (8, 512)
        CARRY_OPS = [0, 1, 2, 10, 11, 12, 13]

        def _build_masks():
            am = np.zeros((NB, NOPS), dtype=bool)
            fm = np.zeros((NB, NOPS), dtype=bool)
            fm[0, :] = True
            for b in range(1, 8):
                am[b, CARRY_OPS] = True
                fm[b, CARRY_OPS] = True
            am[8, [14, 15, 8, 9]] = True
            fm[8, [14, 15, 8, 9]] = True
            for b in range(16, 32):
                fm[b, [3, 4]] = True
            am[32, [10, 11, 12, 13]] = True
            fm[32, [5, 6, 7, 2, 4, 10, 11, 12, 13]] = True
            return (jnp.asarray(am), jnp.asarray(fm))
        key = jax.random.key(seed)
        ks = jax.random.split(key, 9)
        sd = 1.0 / np.sqrt(D)
        sh = 1.0 / np.sqrt(H)
        am, fm = _build_masks()
        return {'x': jax.random.normal(ks[0], (B, S, D), jnp.float32), 'ffn_w1': jax.random.normal(ks[1], (NB, NOPS, D, H), jnp.float32) * sd, 'ffn_b1': jnp.zeros((NB, NOPS, H), jnp.float32), 'ffn_w2': jax.random.normal(ks[2], (NB, NOPS, H, D), jnp.float32) * sh, 'ffn_b2': jnp.zeros((NB, NOPS, D), jnp.float32), 'wq': jax.random.normal(ks[3], (NB, NOPS, D, D), jnp.float32) * sd, 'wk': jax.random.normal(ks[4], (NB, NOPS, D, D), jnp.float32) * sd, 'wv': jax.random.normal(ks[5], (NB, NOPS, D, D), jnp.float32) * sd, 'wo': jax.random.normal(ks[6], (NB, NOPS, D, D), jnp.float32) * sd, 'attn_mask': am, 'ffn_mask': fm}
    _L1_ffn_all = _L1_ffn_setup()
    _L1_ffn_in = {k: v for k, v in _L1_ffn_all.items() if k in ('ffn_w1', 'ffn_b1', 'ffn_w2', 'ffn_b2', 'wq', 'wk', 'wv', 'wo', 'attn_mask', 'ffn_mask')}
    del _L1_ffn_all
    return {'x': x, 'L0_conv_gamma': _L0_conv_in['gamma'], 'L0_conv_beta': _L0_conv_in['beta'], 'L0_conv_W_in': _L0_conv_in['W_in'], 'L0_conv_conv_w': _L0_conv_in['conv_w'], 'L0_conv_conv_b': _L0_conv_in['conv_b'], 'L0_conv_W_x': _L0_conv_in['W_x'], 'L0_conv_W_dt': _L0_conv_in['W_dt'], 'L0_conv_b_dt': _L0_conv_in['b_dt'], 'L0_conv_A_log': _L0_conv_in['A_log'], 'L0_conv_D_skip': _L0_conv_in['D_skip'], 'L0_conv_W_out': _L0_conv_in['W_out'], 'L0_conv_W_p': _L0_conv_in['W_p'], 'L0_conv_b_p': _L0_conv_in['b_p'], 'L0_conv_s1': _L0_conv_in['s1'], 'L0_conv_s2': _L0_conv_in['s2'], 'L1_attn_Wq': _L1_attn_in['Wq'], 'L1_attn_Wk': _L1_attn_in['Wk'], 'L1_attn_Wv': _L1_attn_in['Wv'], 'L1_ffn_ffn_w1': _L1_ffn_in['ffn_w1'], 'L1_ffn_ffn_b1': _L1_ffn_in['ffn_b1'], 'L1_ffn_ffn_w2': _L1_ffn_in['ffn_w2'], 'L1_ffn_ffn_b2': _L1_ffn_in['ffn_b2'], 'L1_ffn_wq': _L1_ffn_in['wq'], 'L1_ffn_wk': _L1_ffn_in['wk'], 'L1_ffn_wv': _L1_ffn_in['wv'], 'L1_ffn_wo': _L1_ffn_in['wo'], 'L1_ffn_attn_mask': _L1_ffn_in['attn_mask'], 'L1_ffn_ffn_mask': _L1_ffn_in['ffn_mask']}

def reference(x, L0_conv_gamma, L0_conv_beta, L0_conv_W_in, L0_conv_conv_w, L0_conv_conv_b, L0_conv_W_x, L0_conv_W_dt, L0_conv_b_dt, L0_conv_A_log, L0_conv_D_skip, L0_conv_W_out, L0_conv_W_p, L0_conv_b_p, L0_conv_s1, L0_conv_s2, L1_attn_Wq, L1_attn_Wk, L1_attn_Wv, L1_ffn_ffn_w1, L1_ffn_ffn_b1, L1_ffn_ffn_w2, L1_ffn_ffn_b2, L1_ffn_wq, L1_ffn_wk, L1_ffn_wv, L1_ffn_wo, L1_ffn_attn_mask, L1_ffn_ffn_mask):
    import jax
    import jax.numpy as jnp

    def _L0_conv_ref(x, gamma, beta, W_in, conv_w, conv_b, W_x, W_dt, b_dt, A_log, D_skip, W_out, W_p, b_p, s1, s2):
        import jax, jax.numpy as jnp
        import numpy as np
        D_CONV = 4
        D_STATE = 16
        GROUP = 8

        def _ln(x, g, b):
            mu = x.mean(-1, keepdims=True)
            v = ((x - mu) ** 2).mean(-1, keepdims=True)
            return (x - mu) * jax.lax.rsqrt(v + 1e-05) * g + b

        def _mamba(x, W_in, conv_w, conv_b, W_x, W_dt, b_dt, A_log, D_skip, W_out):
            B, L, Dm = x.shape
            d_inner = W_in.shape[0] // 2
            dt_rank = W_dt.shape[1]
            xz = x @ W_in.T
            xi, z = (xz[..., :d_inner], xz[..., d_inner:])
            xc = jax.lax.conv_general_dilated(xi.transpose(0, 2, 1), conv_w, (1,), [(D_CONV - 1, 0)], feature_group_count=d_inner, dimension_numbers=('NCH', 'OIH', 'NCH'))
            u = jax.nn.silu((xc + conv_b[:, None]).transpose(0, 2, 1))
            x_dbl = u @ W_x.T
            dt = jax.nn.softplus(x_dbl[..., :dt_rank] @ W_dt.T + b_dt)
            Bs = x_dbl[..., dt_rank:dt_rank + D_STATE]
            Cs = x_dbl[..., dt_rank + D_STATE:]
            A = -jnp.exp(A_log)

            def step(h, inp):
                dt_t, B_t, C_t, u_t = inp
                dA = jnp.exp(dt_t[..., None] * A)
                h = dA * h + (dt_t * u_t)[..., None] * B_t[:, None, :]
                return (h, jnp.einsum('bdn,bn->bd', h, C_t))
            h0 = jnp.zeros((B, d_inner, D_STATE), x.dtype)
            _, ys = jax.lax.scan(step, h0, (dt.transpose(1, 0, 2), Bs.transpose(1, 0, 2), Cs.transpose(1, 0, 2), u.transpose(1, 0, 2)))
            y = ys.transpose(1, 0, 2) + u * D_skip
            return y * jax.nn.silu(z) @ W_out.T
        B, C, W, H = x.shape
        L = W * H
        x_flat = x.reshape(B, C, L).transpose(0, 2, 1)
        x1 = _ln(x_flat, gamma, beta)
        cpg = C // GROUP
        x2 = x.reshape(B, GROUP, cpg, W, H).transpose(0, 2, 1, 3, 4).reshape(B, C, L).transpose(0, 2, 1)
        x2 = _ln(x2, gamma, beta)
        m = lambda t: _mamba(t, W_in, conv_w, conv_b, W_x, W_dt, b_dt, A_log, D_skip, W_out)
        xm = m(x1) + x1 * s1 + (m(x2) + x2 * s2)
        xm = _ln(xm, gamma, beta)
        out = xm @ W_p.T + b_p
        return out.transpose(0, 2, 1).reshape(B, -1, W, H)

    def _L1_attn_ref(x, Wq, Wk, Wv):
        import jax, jax.numpy as jnp
        import numpy as np
        B, T, C = (4, 2048, 64)
        q = jnp.einsum('btc,dc->btd', x, Wq)
        k = jnp.einsum('btc,dc->btd', x, Wk)
        v = jnp.einsum('btc,dc->btd', x, Wv)
        scale = 1.0 / jnp.sqrt(jnp.asarray(x.shape[-1], x.dtype))
        att = jnp.einsum('btd,bsd->bts', q, k) * scale
        causal = jnp.tril(jnp.ones((x.shape[1], x.shape[1]), dtype=bool))
        att = jnp.where(causal[None, :, :], att, -jnp.inf)
        w = jax.nn.softmax(att, axis=-1)
        out = jnp.einsum('bts,bsd->btd', w, v)
        return out

    def _L1_ffn_ref(x, ffn_w1, ffn_b1, ffn_w2, ffn_b2, wq, wk, wv, wo, attn_mask, ffn_mask):
        import jax, jax.numpy as jnp
        import numpy as np
        NB, NOPS = (33, 19)
        D, H = (64, 256)
        B, S = (8, 512)
        CARRY_OPS = [0, 1, 2, 10, 11, 12, 13]

        def _build_masks():
            am = np.zeros((NB, NOPS), dtype=bool)
            fm = np.zeros((NB, NOPS), dtype=bool)
            fm[0, :] = True
            for b in range(1, 8):
                am[b, CARRY_OPS] = True
                fm[b, CARRY_OPS] = True
            am[8, [14, 15, 8, 9]] = True
            fm[8, [14, 15, 8, 9]] = True
            for b in range(16, 32):
                fm[b, [3, 4]] = True
            am[32, [10, 11, 12, 13]] = True
            fm[32, [5, 6, 7, 2, 4, 10, 11, 12, 13]] = True
            return (jnp.asarray(am), jnp.asarray(fm))
        scale = jnp.asarray(1.0 / np.sqrt(D), x.dtype)

        def step(h, p):
            op = jnp.argmax(h[0, 0, :NOPS])
            q = h @ p['wq'][op]
            k = h @ p['wk'][op]
            v = h @ p['wv'][op]
            attn = jax.nn.softmax(jnp.einsum('bqd,bkd->bqk', q, k) * scale, axis=-1)
            y = jnp.einsum('bqk,bkd->bqd', attn, v) @ p['wo'][op]
            h = jnp.where(p['am'][op], y, h)
            z = jax.nn.relu(h @ p['w1'][op] + p['b1'][op]) @ p['w2'][op] + p['b2'][op]
            h = jnp.where(p['fm'][op], z, h)
            return (h, None)
        xs = {'w1': ffn_w1, 'b1': ffn_b1, 'w2': ffn_w2, 'b2': ffn_b2, 'wq': wq, 'wk': wk, 'wv': wv, 'wo': wo, 'am': attn_mask, 'fm': ffn_mask}
        out, _ = jax.lax.scan(step, x, xs)
        return out

    def _gn(v, G=32, eps=1e-05):
        B_, C_, H_, W_ = v.shape
        g = v.reshape(B_, G, C_ // G, H_, W_)
        m = jnp.mean(g, axis=(2, 3, 4), keepdims=True)
        s = jnp.var(g, axis=(2, 3, 4), keepdims=True)
        return ((g - m) / jnp.sqrt(s + eps)).reshape(v.shape)

    def _ln_c(v, eps=1e-06):
        m = jnp.mean(v, axis=1, keepdims=True)
        s = jnp.var(v, axis=1, keepdims=True)
        return (v - m) / jnp.sqrt(s + eps)

    def _ln_t(v, eps=1e-05):
        m = jnp.mean(v, axis=-1, keepdims=True)
        s = jnp.var(v, axis=-1, keepdims=True)
        return (v - m) / jnp.sqrt(s + eps)

    def _to_tokens(v):
        B_, C_, H_, W_ = v.shape
        return v.reshape(B_, C_, H_ * W_).transpose(0, 2, 1)

    def _from_tokens(t, like):
        B_, C_, H_, W_ = like.shape
        return t.transpose(0, 2, 1).reshape(B_, C_, H_, W_)
    x = x + _L0_conv_ref(_gn(x), L0_conv_gamma, L0_conv_beta, L0_conv_W_in, L0_conv_conv_w, L0_conv_conv_b, L0_conv_W_x, L0_conv_W_dt, L0_conv_b_dt, L0_conv_A_log, L0_conv_D_skip, L0_conv_W_out, L0_conv_W_p, L0_conv_b_p, L0_conv_s1, L0_conv_s2)
    t = _to_tokens(x)
    t = t + _L1_attn_ref(_ln_t(t), L1_attn_Wq, L1_attn_Wk, L1_attn_Wv)
    t = t + _L1_ffn_ref(_ln_t(t), L1_ffn_ffn_w1, L1_ffn_ffn_b1, L1_ffn_ffn_w2, L1_ffn_ffn_b2, L1_ffn_wq, L1_ffn_wk, L1_ffn_wv, L1_ffn_wo, L1_ffn_attn_mask, L1_ffn_ffn_mask)
    x = _from_tokens(t, x)
    return x

_drawn_inputs = setup_inputs


def setup_inputs(seed=0):
    import zlib

    import numpy as np

    out = dict(_drawn_inputs(seed))
    spreads = {'L0_conv_gamma': (1.0, 0.2),
     'L0_conv_beta': (0.0, 0.1),
     'L0_conv_conv_b': (0.0, 0.8),
     'L0_conv_D_skip': (1.0, 0.6),
     'L0_conv_b_p': (0.0, 0.1),
     'L1_ffn_ffn_b1': (0.0, 0.1),
     'L1_ffn_ffn_b2': (0.0, 0.1)}
    factors = {'L0_conv_W_in': 8.0,
     'L0_conv_conv_w': 8.0,
     'L0_conv_W_x': 8.0,
     'L0_conv_W_dt': 8.0,
     'L0_conv_b_dt': 8.0,
     'L0_conv_A_log': 8.0,
     'L0_conv_W_out': 8.0,
     'L1_ffn_wq': 4.945,
     'L1_ffn_wk': 4.669}
    for name, (base, spread) in spreads.items():
        noise = np.random.default_rng([zlib.crc32(name.encode()), seed]).standard_normal(out[name].shape)
        drawn = base * np.exp(spread * noise) if base else spread * noise
        out[name] = jnp.asarray(drawn.astype(out[name].dtype))
    for name, factor in factors.items():
        out[name] = (out[name] * factor).astype(out[name].dtype)
    return out
```

```python
import concourse.bass as bass
from concourse import mybir
from contextlib import ExitStack

FP32 = mybir.dt.float32
BF16 = mybir.dt.bfloat16
I32 = mybir.dt.int32
U32 = mybir.dt.uint32
U8 = mybir.dt.uint8
ALU = mybir.AluOpType
ACT = mybir.ActivationFunctionType
AX = mybir.AxisListType

B, C, L = 4, 64, 1024
DI, NS, DR = 128, 16, 4
NSEQ = 2 * B
NSTEP, NOPS, HID = 33, 19, 256
XW = L + 4
HALF = 512
T2C = 2 * L
VW = 66
EPS = 1e-5
SCALE = float(C) ** -0.5
IDN, PAIR, CEN, MEAN, CAUS, SELV, IOTA = 0, 128, 256, 384, 512, 640, 672
CONSTW = IOTA + 72
MASKW = -(-NSTEP * NOPS // 4)


def atleast(eng, sem, value):
    if not isinstance(value, int) or value > 0:
        eng.wait_ge(sem, value)


def settle(eng, sem, value, passed):
    eng.wait_ge(sem, value)
    eng.sem_inc(passed, 1)


def build_prepare(nc, w, inp):
    ctx = ExitStack()
    with ctx:
        def sb(name, shape, dt=FP32):
            return ctx.enter_context(nc.sbuf_tensor(name, shape, dt))

        def sem(name):
            return ctx.enter_context(nc.semaphore(name))

        xx = sb("xx", [128, B * L])
        win = sb("win", [128, 2, C])
        conv_w = sb("conv_w", [128, 4])
        nat = sb("nat", [128, 11, 128])
        NCA, NCB, NG, NBC, NDT, NO, NP, NQ, NK, NV, NX = range(11)
        wdtT = sb("wdtT", [128, 128])
        a_log = sb("a_log", [128, NS])
        stats = sb("stats", [128, B, 2, 6])
        mv = sb("mv", [128, B, 2])
        gstat = sb("gstat", [128, 2, B])
        gdev = sb("gdev", [128, B])
        grs = sb("grs", [128, B])
        z0 = sb("z0", [128, L])
        sq = sb("sq", [128, L])
        sd = sb("sd", [128, L])
        rs = sb("rs", [128, L])
        zt = sb("zt", [128, L])
        pw = [ctx.enter_context(nc.psum_tensor(f"pw{i}", [128, HALF], FP32)) for i in range(2)]
        pg = ctx.enter_context(nc.psum_tensor("pg", [128, HALF], FP32))
        pd = ctx.enter_context(nc.psum_tensor("pd", [128, L], FP32))
        pv = ctx.enter_context(nc.psum_tensor("pv", [128, L], FP32))

        zeroed, x_in, w_in, act_w_in = sem("zeroed"), sem("x_in"), sem("w_in"), sem("act_w_in")
        scaled, turned, weight_out = sem("scaled"), sem("turned"), sem("weight_out")
        a_exp, stats_done, aggr_done, pair_done = sem("a_exp"), sem("stats_done"), sem("aggr_done"), sem("pair_done")
        gn_chain, gsd_done, grs_done = sem("gn_chain"), sem("gsd_done"), sem("grs_done")
        z0_done, dev_done, sq_done, var_done = sem("z0_done"), sem("dev_done"), sem("sq_done"), sem("var_done")
        sd_done, rs_done, zt_done, dve_x, act_x = sem("sd_done"), sem("rs_done"), sem("zt_done"), sem("dve_x"), sem("act_x")
        sel_done, code_chain = sem("sel_done"), sem("code_chain")
        mask_words = sb("mask_words", [1, 2, MASKW], I32)
        mask_bytes = mask_words[:, :, :].bitcast(U8)
        flags = sb("flags", [1, 2, NSTEP * NOPS])

        cst = w["cst"]
        block = ctx.enter_context(nc.Block())

        @block.sync
        def _(sp):
            sp.dma_start(cst[:, :], inp["consts"]).then_inc(w_in, 16)
            xd = inp["x"].rearrange("b c h w -> c b (h w)")
            sp.dma_start(xx[0:C, :].rearrange("c (b t) -> c b t", b=B), xd).then_inc(x_in, 16)
            xg = inp["x"].rearrange("b (g j) h w -> j g b (h w)", j=8)
            for j in range(8):
                sp.dma_start(xx[C + 8 * j:C + 8 * j + 8, :].rearrange("g (b t) -> g b t", b=B),
                             xg[j, :, :, :]).then_inc(x_in, 16)
            sp.dma_start(win[:, :, :], inp["W_in"].rearrange("(j d) c -> d j c", j=2)).then_inc(w_in, 16)
            sp.dma_start(conv_w[:, :], inp["conv_w"].rearrange("d a k -> d (a k)")).then_inc(w_in, 16)
            for half in range(2):
                sp.dma_start(w["gam"][C * half:C * half + C, :], inp["gamma"].rearrange("(c a) -> c a", a=1)).then_inc(w_in, 16)
                sp.dma_start(w["bet"][C * half:C * half + C, :], inp["beta"].rearrange("(c a) -> c a", a=1)).then_inc(w_in, 16)
            for r in range(2):
                sp.dma_start(w["xst"][C * r:C * r + C, :].rearrange("c (p t) -> c p t", p=2),
                             inp["x"].rearrange("(p r) c h w -> r c p (h w)", r=2)[r, :, :, :]).then_inc(x_in, 16)

        @block.gpsimd
        def _(pool):
            nc.gpsimd.memset(nat[:, :, :], 0.0).then_inc(zeroed, 1)
            nc.gpsimd.memset(w["eps"][:, :], EPS).then_inc(zeroed, 1)
            nc.gpsimd.memset(w["xs"][:, :], 0.0).then_inc(zeroed, 1)
            nc.gpsimd.memset(w["res"][:, :, :], 0.0).then_inc(zeroed, 1)
            n = NSTEP * NOPS
            nc.gpsimd.memset(w["code"][:, n:], 1000.0).then_inc(code_chain, 1)
            pool.wait_ge(w_in, 16 * 7)
            pool.wait_ge(act_w_in, 16 * 25)
            nc.gpsimd.tensor_copy(flags[:, :, :], mask_bytes[:, :, 0:NSTEP * NOPS]).then_inc(code_chain, 1)
            pool.wait_ge(code_chain, 2)
            nc.gpsimd.tensor_scalar(flags[:, 1, :], flags[:, 1, :], 2.0, None, ALU.mult).then_inc(code_chain, 1)
            pool.wait_ge(code_chain, 3)
            nc.gpsimd.tensor_tensor(flags[:, 0, :], flags[:, 0, :], flags[:, 1, :], ALU.add).then_inc(code_chain, 1)
            pool.wait_ge(code_chain, 4)
            nc.gpsimd.tensor_scalar(flags[:, 1, :], flags[:, 0, :], 0.0, 1000.0, ALU.is_equal, ALU.mult).then_inc(code_chain, 1)
            pool.wait_ge(code_chain, 5)
            nc.gpsimd.tensor_tensor(flags[:, 0, :], flags[:, 0, :], flags[:, 1, :], ALU.add).then_inc(code_chain, 1)
            pool.wait_ge(code_chain, 6)
            nc.gpsimd.tensor_tensor(w["code"][:, 0:n].rearrange("a (b o) -> a b o", o=NOPS),
                                    flags[:, 0, :].rearrange("a (b o) -> a b o", o=NOPS),
                                    cst[0:1, IOTA:IOTA + NSTEP].unsqueeze(2).broadcast_to((1, NSTEP, NOPS)), ALU.add).then_inc(code_chain, 1)

        @block.scalar
        def _(act):
            act.wait_ge(zeroed, 1)
            for j, row in ((0, 0), (2, 64), (3, 96), (1, 32)):
                act.dma_start(nat[row:row + 32, NBC, :], inp["W_x"][DR:DR + 32, :]).then_inc(act_w_in, 16)
            act.dma_start(nat[0:DR, NX, :], inp["W_x"][0:DR, :]).then_inc(act_w_in, 16)
            act.dma_start(nat[:, NDT, 0:DR], inp["W_dt"]).then_inc(act_w_in, 16)
            act.dma_start(nat[0:C, NO, :], inp["W_out"]).then_inc(act_w_in, 16)
            act.dma_start(a_log[:, :], inp["A_log"]).then_inc(act_w_in, 16)
            act.dma_start(w["cb"][:, :], inp["conv_b"].rearrange("(d a) -> d a", a=1)).then_inc(act_w_in, 16)
            act.dma_start(w["bdt"][:, :], inp["b_dt"].rearrange("(d a) -> d a", a=1)).then_inc(act_w_in, 16)
            act.dma_start(w["dsk"][:, :], inp["D_skip"].rearrange("(d a) -> d a", a=1)).then_inc(act_w_in, 16)
            for i, name in ((0, "s1"), (1, "s2")):
                act.dma_start(w["scol"][:, i:i + 1], inp[name].rearrange("(a c) -> a c", a=1).broadcast_to((128, 1))).then_inc(act_w_in, 16)
            act.dma_start(mask_words[:, 0, :], inp["attn_mask"].rearrange("(a w) -> a w", a=1)).then_inc(act_w_in, 16)
            act.dma_start(mask_words[:, 1, :], inp["ffn_mask"].rearrange("(a w) -> a w", a=1)).then_inc(act_w_in, 16)
            for r in range(2):
                s = slice(C * r, C * r + C)
                for slot, name in ((NP, "W_p"), (NQ, "Wq"), (NK, "Wk"), (NV, "Wv")):
                    act.dma_start(nat[s, slot, s], inp[name]).then_inc(act_w_in, 16)
                act.dma_start(w["bp"][s, :], inp["b_p"].rearrange("(c a) -> c a", a=1)).then_inc(act_w_in, 16)
            act.wait_ge(act_w_in, 16 * 25)
            nc.scalar.activation(a_log[:, :], a_log[:, :], ACT.Exp).then_inc(a_exp, 1)
            act.wait_ge(gn_chain, 4)
            act.wait_ge(zeroed, 2)
            nc.scalar.activation(gdev[:, :], gdev[:, :], ACT.Ln, bias=w["eps"][:, :]).then_inc(gsd_done, 1)
            act.wait_ge(gsd_done, 1)
            nc.scalar.activation(grs[:, :], gdev[:, :], ACT.Exp, scale=-0.5).then_inc(grs_done, 1)
            act.wait_ge(w_in, 16 * 7)
            for b in range(B):
                act.wait_ge(dev_done, b + 1)
                atleast(act, var_done, b)
                nc.scalar.activation(sq[:, :], pd[:, :], ACT.Square).then_inc(sq_done, 1)
                act.wait_ge(var_done, b + 1)
                atleast(act, rs_done, b)
                nc.scalar.activation(sd[:, :], pv[:, :], ACT.Ln, bias=w["eps"][:, :]).then_inc(sd_done, 1)
                act.wait_ge(sd_done, b + 1)
                atleast(act, zt_done, b)
                nc.scalar.activation(rs[:, :], sd[:, :], ACT.Exp, scale=-0.5).then_inc(rs_done, 1)
                act.wait_ge(zt_done, b + 1)
                act.wait_ge(zeroed, 3)
                plain, shuffled = b * XW, (B + b) * XW
                nc.scalar.activation(w["xs"][C:128, plain + 4:plain + 4 + L], zt[0:C, :], ACT.Identity,
                                     bias=w["bet"][0:C, :], scale=w["gam"][0:C, :])
                nc.scalar.activation(w["xs"][0:C, shuffled + 3:shuffled + 3 + L], zt[C:128, :], ACT.Identity,
                                     bias=w["bet"][C:128, :], scale=w["gam"][C:128, :]).then_inc(act_x, 1)

        turns = [(NCA, w["wca"], 1.0), (NCB, w["wcb"], 1.0), (NG, w["wg"], 1.0), (NBC, w["wbc"], 0.5),
                 (NDT, wdtT, 1.0), (NO, w["wo"], 0.25), (NP, w["wp"], 1.0), (NQ, w["wq1"], 1.0),
                 (NK, w["wk1"], 1.0), (NV, w["wv1"], 1.0)]

        @block.vector
        def _(dve):
            dve.wait_ge(x_in, 16 * 11)
            for b in range(B):
                for h in range(2):
                    nc.vector.bn_stats(stats[:, b, h, :], xx[:, b * L + h * HALF:b * L + (h + 1) * HALF]).then_inc(stats_done, 1)
            dve.wait_ge(stats_done, 2 * B)
            for b in range(B):
                nc.vector.bn_aggr(mv[:, b, :], stats[:, b, :, :].rearrange("p h s -> p (h s)")).then_inc(aggr_done, 1)
            dve.wait_ge(pair_done, 1)
            nc.vector.tensor_copy(gstat[:, :, :], pg[:, 0:2 * B].rearrange("p (b s) -> p s b", s=2)).then_inc(gn_chain, 1)
            dve.wait_ge(gn_chain, 1)
            nc.vector.tensor_tensor(gdev[:, :], mv[:, :, 0], gstat[:, 0, :], ALU.subtract).then_inc(gn_chain, 1)
            dve.wait_ge(gn_chain, 2)
            nc.vector.tensor_tensor(gdev[:, :], gdev[:, :], gdev[:, :], ALU.mult).then_inc(gn_chain, 1)
            dve.wait_ge(gn_chain, 3)
            nc.vector.tensor_tensor(gdev[:, :], gdev[:, :], gstat[:, 1, :], ALU.add).then_inc(gn_chain, 1)
            dve.wait_ge(grs_done, 1)
            dve.wait_ge(w_in, 16 * 7)
            for b in range(B):
                atleast(dve, dev_done, b)
                nc.vector.tensor_scalar(z0[:, :], xx[:, b * L:(b + 1) * L], gstat[:, 0, b:b + 1], grs[:, b:b + 1],
                                        ALU.subtract, ALU.mult).then_inc(z0_done, 1)
                dve.wait_ge(rs_done, b + 1)
                atleast(dve, dve_x, 2 * b)
                atleast(dve, act_x, b)
                nc.vector.tensor_tensor(zt[:, :], pd[:, :], rs[:, :], ALU.mult).then_inc(zt_done, 1)
                dve.wait_ge(zt_done, b + 1)
                dve.wait_ge(zeroed, 3)
                plain, shuffled = b * XW, (B + b) * XW
                nc.vector.tensor_scalar(w["xs"][0:C, plain + 3:plain + 3 + L], zt[0:C, :], w["gam"][0:C, :],
                                        w["bet"][0:C, :], ALU.mult, ALU.add).then_inc(dve_x, 1)
                nc.vector.tensor_scalar(w["xs"][C:128, shuffled + 4:shuffled + 4 + L], zt[C:128, :], w["gam"][C:128, :],
                                        w["bet"][C:128, :], ALU.mult, ALU.add).then_inc(dve_x, 1)
            dve.wait_ge(zeroed, 1)
            for slot, lo, hi in ((NCA, 3, 2), (NCB, 1, 0)):
                for part, tap in ((0, lo), (1, hi)):
                    nc.vector.tensor_scalar(nat[:, slot, C * part:C * part + C], win[:, 0, :],
                                            conv_w[:, tap:tap + 1], None, ALU.mult).then_inc(scaled, 1)
            nc.vector.tensor_copy(nat[:, NG, 0:C], win[:, 1, :]).then_inc(scaled, 1)
            for n, (slot, to, by) in enumerate(turns):
                dve.wait_ge(turned, n + 1)
                nc.vector.tensor_scalar(to[:, :], pw[n % 2][:, 0:128], by, None, ALU.mult).then_inc(weight_out, 1)
            dve.wait_ge(turned, len(turns) + 1)
            nc.vector.tensor_scalar(w["wdt"][:, :], pw[0][:, 0:128], 0.5, None, ALU.mult).then_inc(weight_out, 1)
            dve.wait_ge(a_exp, 1)
            nc.vector.tensor_scalar(w["aneg"][:, :], a_log[:, :], -1.0, None, ALU.mult)
            nc.vector.tensor_scalar(w["hcb"][:, :], w["cb"][:, :], 0.5, None, ALU.mult)
            dve.wait_ge(zeroed, 4)
            for i in range(2):
                nc.vector.tensor_scalar(w["res"][:, i, 0:C], cst[:, IDN:IDN + C], w["scol"][:, i:i + 1], None, ALU.mult)
            nc.vector.tensor_copy(w["sel"][:, :, :], cst[:, SELV:SELV + 32].unsqueeze(2).broadcast_to((128, 32, 128))).then_inc(sel_done, 1)

        @block.tensor
        def _(pe):
            pe.wait_ge(w_in, 16)
            pe.wait_ge(aggr_done, B)
            nc.tensor.matmul(pg[:, 0:2 * B], cst[:, PAIR:PAIR + 128], mv[:, :, :].rearrange("p b s -> p (b s)"),
                             start=True, stop=True).then_inc(pair_done, 1)
            for b in range(B):
                pe.wait_ge(z0_done, b + 1)
                atleast(pe, zt_done, b)
                for h in range(2):
                    last = nc.tensor.matmul(pd[:, h * HALF:(h + 1) * HALF], cst[:, CEN:CEN + 128],
                                            z0[:, h * HALF:(h + 1) * HALF], start=True, stop=True)
                last.then_inc(dev_done, 1)
                pe.wait_ge(sq_done, b + 1)
                atleast(pe, sd_done, b)
                for h in range(2):
                    last = nc.tensor.matmul(pv[:, h * HALF:(h + 1) * HALF], cst[:, MEAN:MEAN + 128],
                                            sq[:, h * HALF:(h + 1) * HALF], start=True, stop=True)
                last.then_inc(var_done, 1)
            pe.wait_ge(scaled, 5)
            pe.wait_ge(act_w_in, 16 * 25)
            for n, (slot, _, _) in enumerate(turns):
                atleast(pe, weight_out, n - 1)
                nc.tensor.transpose(pw[n % 2][:, 0:128], nat[:, slot, :], cst[:, IDN:IDN + 128]).then_inc(turned, 1)
            pe.wait_ge(weight_out, len(turns))
            nc.tensor.matmul(pw[0][:, 0:128], nat[:, NX, :], wdtT[:, :], start=True, stop=True).then_inc(turned, 1)


def build_scan(nc, w, inp):
    ctx = ExitStack()
    with ctx:
        def sb(name, shape, dt=FP32):
            return ctx.enter_context(nc.sbuf_tensor(name, shape, dt))

        def ps(name, shape):
            return ctx.enter_context(nc.psum_tensor(name, shape, FP32))

        def sem(name):
            return ctx.enter_context(nc.semaphore(name))

        u2 = [sb(f"u2_{i}", [DI, L]) for i in range(2)]
        gate = [sb(f"gate_{i}", [DI, L]) for i in range(2)]
        dt = [sb(f"dt_{i}", [DI, L]) for i in range(2)]
        dtu = [sb(f"dtu_{i}", [DI, L]) for i in range(2)]
        bc3 = [sb(f"bc3_{i}", [128, L], BF16) for i in range(2)]
        yg = [sb(f"yg_{i}", [DI, L]) for i in range(2)]
        da = [sb(f"da_{i}", [DI, L]) for i in range(2)]
        cc = [sb(f"cc_{i}", [DI, L]) for i in range(2)]
        hh = [sb(f"hh_{i}", [DI, L]) for i in range(2)]
        hc = [sb(f"hc_{i}", [DI, L]) for i in range(2)]
        th, xb = sb("th", [DI, L]), sb("xb", [DI, L])
        th2, xb2 = sb("th2", [DI, L]), sb("xb2", [DI, L])
        ex, one = sb("ex", [DI, L]), sb("one", [DI, L])
        ln, rl = sb("ln", [DI, L]), sb("rl", [DI, L])
        rest, yt = sb("rest", [128, L]), sb("yt", [DI, L])

        pb = [ps(f"pb_{i}", [DI, L]) for i in range(2)]
        pc = ps("pc", [DI, HALF])
        px = ps("px", [128, HALF])
        py = ps("py", [DI, L])

        b_full, c_full, c_out = sem("b_full"), sem("c_full"), sem("c_out")
        dbu_done, da_done, scan_done = sem("dbu_done"), sem("da_done"), sem("scan_done")
        hc_done, hc_used, y_free, yg_done = sem("hc_done"), sem("hc_used"), sem("y_free"), sem("yg_done")
        px_full, px_free = sem("px_full"), sem("px_free")
        u_done, g_done, e_done, one_done, lost_done, part_done, l_done, dt_done, dtu_done = (
            sem("u_done"), sem("g_done"), sem("e_done"), sem("one_done"), sem("lost_done"), sem("part_done"),
            sem("l_done"), sem("dt_done"), sem("dtu_done"))
        bc1_done, bc_chain = sem("bc1_done"), sem("bc_chain")
        xm_done, stacked = sem("xm_done"), sem("stacked")
        BC_OPS = 3
        PIECES = 8
        ident, xs = w["cst"][:, IDN:IDN + 128], w["xs"]

        def half(h):
            return slice(h * HALF, (h + 1) * HALF)

        def use(q, piece, out_before):
            return PIECES * q + piece + 2 * out_before

        block = ctx.enter_context(nc.Block())
        pool_passed = sem("pool_passed")

        def pe_piece(pe, q, b, s, out_before, piece):
            kind, h, par = piece // 2, piece % 2, s
            k = use(q, piece, out_before)
            atleast(pe, px_free, k)
            at = (s * B + b) * XW + h * HALF
            if kind == 0:
                nc.tensor.matmul(px[:, :], w["wca"][:, :], xs[:, bass.ds(at + 3, HALF)], start=True, stop=False)
                last = nc.tensor.matmul(px[:, :], w["wcb"][:, :], xs[:, bass.ds(at + 1, HALF)], start=False, stop=True)
            elif kind == 1:
                last = nc.tensor.matmul(px[:, :], w["wg"][:, :], xs[:, bass.ds(at + 3, HALF)], start=True, stop=True)
            else:
                pe.wait_ge(u_done, 2 * q + h + 1)
                last = nc.tensor.matmul(px[:, :], (w["wdt"] if kind == 2 else w["wbc"])[:, :], u2[par][:, half(h)],
                                        start=True, stop=True)
            last.then_inc(px_full, 1)

        def pe_b(pe, u, n, par, q):
            if n == 0:
                pe.wait_ge(bc_chain, BC_OPS * (q + 1))
            atleast(pe, scan_done, u - 1)
            for h in range(2):
                last = nc.tensor.matmul(pb[n % 2][:, half(h)], w["sel"][:, n, :], bc3[par][:, half(h)], start=True, stop=True)
            last.then_inc(b_full, 1)

        def pe_c(pe, u, n, par, h):
            atleast(pe, c_out, 2 * u + h)
            nc.tensor.matmul(pc[:, :], w["sel"][:, NS + n, :], bc3[par][:, half(h)], start=True, stop=True).then_inc(c_full, 1)

        def pe_sum(pe, u, n, q, h):
            if h == 0:
                pe.wait_ge(hc_done, u + 1)
            if n == 0:
                atleast(pe, y_free, 2 * q - 1 + h)
            nc.tensor.matmul(py[:, half(h)], ident, hc[n % 2][:, half(h)], start=(n == 0), stop=(n == NS - 1)).then_inc(hc_used, 1)

        def pe_out(pe, b, h, k):
            atleast(pe, px_free, k)
            pe.wait_ge(yg_done, 2 * b + 2)
            for s in range(2):
                nc.tensor.matmul(px[:, :], w["wo"][:, :], yg[s][:, half(h)], start=(s == 0), stop=False)
            for s in range(2):
                last = nc.tensor.matmul(px[:, :], w["res"][:, s, :], xs[:, bass.ds((s * B + b) * XW + 3 + h * HALF, HALF)],
                                        start=False, stop=(s == 1))
            last.then_inc(px_full, 1)

        def pe_units(pe, b, s, first=False, nxt=None, out=None):
            q, par = 2 * b + s, s
            for n in range(NS):
                u = NS * q + n
                m = (n - 2) % NS
                late = not (first and n < 2)
                pe_c(pe, u, n, par, 0)
                if late:
                    pe_sum(pe, u - 2, m, q if n >= 2 else q - 1, 0)
                if n < NS - 1:
                    pe_b(pe, u + 1, n + 1, par, q)
                elif nxt:
                    pe_b(pe, u + 1, 0, nxt[1], q + 1)
                pe_c(pe, u, n, par, 1)
                if late:
                    pe_sum(pe, u - 2, m, q if n >= 2 else q - 1, 1)
                if nxt and 1 <= n <= PIECES:
                    pe_piece(pe, 2 * nxt[0] + nxt[1], *nxt, n - 1)
                if out and n in (11, 12):
                    pe_out(pe, out[0], n - 11, out[1] + n - 11)

        @block.tensor
        def _(pe):
            for piece in range(PIECES):
                pe_piece(pe, 0, 0, 0, 0, piece)
            pe_b(pe, 0, 0, 0, 0)
            pe_units(pe, 0, 0, first=True, nxt=(0, 1, 0))
            with pe.Fori(0, B - 1) as b:
                pe_units(pe, b, 1, nxt=(b + 1, 0, b))
                pe_units(pe, b + 1, 0, nxt=(b + 1, 1, b), out=(b, use(2 * b + 4, 0, b)))
            b = B - 1
            pe_units(pe, b, 1)
            u = NS * NSEQ
            for back in (2, 1):
                for h in range(2):
                    pe_sum(pe, u - back, NS - back, NSEQ - 1, h)
            for h in range(2):
                pe_out(pe, b, h, use(NSEQ, 0, b) + h)

        def act_piece(act, q, par, out_before, piece):
            kind, h = piece // 2, piece % 2
            k = use(q, piece, out_before)
            act.wait_ge(px_full, k + 1)
            if kind == 0:
                atleast(act, u_done, 2 * q + h - 1)
                nc.scalar.activation(th[:, half(h)], px[:, :], ACT.Tanh, bias=w["hcb"][:, :], scale=0.5)
                nc.scalar.activation(xb[:, half(h)], px[:, :], ACT.Identity, bias=w["cb"][:, :]).then_inc(px_free, 1)
            elif kind == 1:
                atleast(act, g_done, 2 * q + h - 1)
                nc.scalar.activation(th2[:, half(h)], px[:, :], ACT.Tanh, scale=0.5)
                nc.scalar.activation(xb2[:, half(h)], px[:, :], ACT.Identity).then_inc(px_free, 1)
            elif kind == 2:
                atleast(act, dt_done, q)
                nc.scalar.activation(ex[:, half(h)], px[:, :], ACT.Abs, bias=w["bdt"][:, :])
                nc.scalar.activation(rl[:, half(h)], px[:, :], ACT.Relu, bias=w["bdt"][:, :]).then_inc(px_free, 1)
            else:
                nc.scalar.activation(bc3[par][:, half(h)], px[:, :], ACT.Copy).then_inc(bc1_done, 1)

        def act_one(act, q, out_before, h):
            act.wait_ge(px_free, use(q, 4 + h, out_before) + 1)
            nc.scalar.activation(ex[:, half(h)], ex[:, half(h)], ACT.Exp, scale=-1.0).then_inc(e_done, 1)
            act.wait_ge(e_done, 2 * q + h + 1)
            nc.scalar.activation(one[:, half(h)], ex[:, half(h)], ACT.Identity, bias=1.0).then_inc(one_done, 1)

        def act_ln(act, q):
            act.wait_ge(one_done, 2 * q + 2)
            nc.scalar.activation(ln[:, :], one[:, :], ACT.Ln).then_inc(l_done, 1)

        def act_exp(act, u, n, par, q):
            if n == 0:
                act.wait_ge(dt_done, q + 1)
            atleast(act, scan_done, u - 1)
            nc.scalar.activation(da[n % 2][:, :], dt[par][:, :], ACT.Exp, scale=w["aneg"][:, n:n + 1]).then_inc(da_done, 1)

        def act_c(act, u, n, h):
            act.wait_ge(c_full, 2 * u + h + 1)
            if h == 0:
                atleast(act, hc_done, u - 1)
            nc.scalar.activation(cc[n % 2][:, half(h)], pc[:, :], ACT.Copy).then_inc(c_out, 1)

        def act_out(act, b, h, k):
            act.wait_ge(px_full, k + 1)
            nc.scalar.activation(w["xm"][:, bass.ds(b * L + h * HALF, HALF)], px[0:C, :], ACT.Copy).then_inc(px_free, 1)

        def act_units(act, b, s, nxt=None, out=None):
            q, par = 2 * b + s, s
            for n in range(NS):
                u = NS * q + n
                act_c(act, u, n, 0)
                if nxt and 2 <= n <= PIECES + 1:
                    act_piece(act, 2 * nxt[0] + nxt[1], nxt[1], nxt[2], n - 2)
                if out and n in (12, 13):
                    act_out(act, out[0], n - 12, out[1] + n - 12)
                act_c(act, u, n, 1)
                if n < NS - 1:
                    act_exp(act, u + 1, n + 1, par, q)
                elif nxt:
                    act_exp(act, u + 1, 0, nxt[1], q + 1)
                if nxt and n in (6, 7):
                    act_one(act, 2 * nxt[0] + nxt[1], nxt[2], n - 6)
                if nxt and n == 10:
                    act_ln(act, 2 * nxt[0] + nxt[1])

        @block.scalar
        def _(act):
            for piece in range(PIECES):
                act_piece(act, 0, 0, 0, piece)
                if piece in (4, 5):
                    act_one(act, 0, 0, piece - 4)
            act_ln(act, 0)
            act_exp(act, 0, 0, 0, 0)
            act_units(act, 0, 0, nxt=(0, 1, 0))
            with act.Fori(0, B - 1) as b:
                act_units(act, b, 1, nxt=(b + 1, 0, b))
                act_units(act, b + 1, 0, nxt=(b + 1, 1, b), out=(b, use(2 * b + 4, 0, b)))
            b = B - 1
            act_units(act, b, 1)
            for h in range(2):
                act_out(act, b, h, use(NSEQ, 0, b) + h)
            act.drain().then_inc(xm_done, 1)

        def dve_piece(dve, q, par, out_before, piece):
            kind, h = piece // 2, piece % 2
            k = use(q, piece, out_before)
            if kind == 0:
                dve.wait_ge(px_free, k + 1)
                atleast(dve, yg_done, q - 1)
                nc.vector.scalar_tensor_tensor(u2[par][:, half(h)], th[:, half(h)], 1.0, xb[:, half(h)],
                                               ALU.add, ALU.mult).then_inc(u_done, 1)
            elif kind == 1:
                dve.wait_ge(px_free, k + 1)
                atleast(dve, yg_done, q - 1)
                nc.vector.scalar_tensor_tensor(gate[par][:, half(h)], th2[:, half(h)], 1.0, xb2[:, half(h)],
                                               ALU.add, ALU.mult).then_inc(g_done, 1)
            elif kind == 3:
                dve.wait_ge(bc1_done, 2 * q + h + 1)
                if h == 0:
                    atleast(dve, bc_chain, BC_OPS * q)
                nc.vector.tensor_tensor(rest[64:128, half(h)], px[64:128, :], bc3[par][64:128, half(h)],
                                        ALU.subtract).then_inc(px_free, 1)

        def dve_lost(dve, q):
            dve.wait_ge(one_done, 2 * q + 2)
            nc.vector.scalar_tensor_tensor(ex[:, :], one[:, :], 1.0, ex[:, :], ALU.subtract, ALU.subtract).then_inc(lost_done, 1)

        def dve_parts(dve, q, par, out_before):
            dve.wait_ge(px_free, use(q, PIECES - 1, out_before) + 1)
            base = BC_OPS * q
            nc.vector.tensor_copy(bc3[par][64:128, :], rest[64:128, :]).then_inc(bc_chain, 1)
            dve.wait_ge(bc_chain, base + 1)
            nc.vector.tensor_tensor(rest[96:128, :], rest[96:128, :], bc3[par][96:128, :], ALU.subtract).then_inc(bc_chain, 1)
            dve.wait_ge(bc_chain, base + 2)
            nc.vector.tensor_copy(bc3[par][96:128, :], rest[96:128, :]).then_inc(bc_chain, 1)

        def dve_dt(dve, q, par):
            dve.wait_ge(l_done, q + 1)
            dve.wait_ge(part_done, q + 1)
            atleast(dve, da_done, NS * (q - 1))
            nc.vector.tensor_tensor(dt[par][:, :], ln[:, :], rl[:, :], ALU.add).then_inc(dt_done, 1)

        def dve_dtu(dve, q, par):
            dve.wait_ge(dt_done, q + 1)
            atleast(dve, dbu_done, NS * (q - 1))
            nc.vector.tensor_tensor(dtu[par][:, :], dt[par][:, :], u2[par][:, :], ALU.mult).then_inc(dtu_done, 1)

        def dve_unit(dve, u, n, par, q):
            dve.wait_ge(b_full, u + 1)
            if n == 0:
                dve.wait_ge(dtu_done, q + 1)
            nc.vector.tensor_tensor(pb[n % 2][:, :], pb[n % 2][:, :], dtu[par][:, :], ALU.mult).then_inc(dbu_done, 1)
            dve.wait_ge(da_done, u + 1)
            dve.wait_ge(dbu_done, u + 1)
            atleast(dve, hc_done, u - 1)
            nc.vector.tensor_tensor_scan(hh[n % 2][:, :], da[n % 2][:, :], pb[n % 2][:, :], 0.0,
                                         ALU.mult, ALU.add).then_inc(scan_done, 1)

        def dve_y(dve, q, s, h):
            dve.wait_ge(hc_used, 2 * NS * (q + 1) - 1 + h)
            if h == 0:
                atleast(dve, yg_done, q)
            nc.vector.scalar_tensor_tensor(yt[:, half(h)], u2[s][:, half(h)], w["dsk"][:, :], py[:, half(h)],
                                           ALU.mult, ALU.add).then_inc(y_free, 1)

        def dve_units(dve, b, s, nxt=None, prev=None):
            q, par = 2 * b + s, s
            for n in range(NS):
                u = NS * q + n
                if prev and n == 2:
                    for h in range(2):
                        dve_y(dve, q - 1, prev[1], h)
                dve_unit(dve, u, n, par, q)
                if nxt:
                    qn = 2 * nxt[0] + nxt[1]
                    if 3 <= n <= 6:
                        dve_piece(dve, qn, nxt[1], nxt[2], n - 3)
                    if n in (8, 9):
                        dve_piece(dve, qn, nxt[1], nxt[2], n - 2)
                    if n == 8:
                        dve_lost(dve, qn)
                    if n == 10:
                        dve_parts(dve, qn, nxt[1], nxt[2])
                    if n == 12:
                        dve_dt(dve, qn, nxt[1])
                    if n == 13:
                        dve_dtu(dve, qn, nxt[1])

        @block.vector
        def _(dve):
            for piece in range(PIECES):
                dve_piece(dve, 0, 0, 0, piece)
            dve_lost(dve, 0)
            dve_parts(dve, 0, 0, 0)
            dve_dt(dve, 0, 0)
            dve_dtu(dve, 0, 0)
            dve_units(dve, 0, 0, nxt=(0, 1, 0))
            with dve.Fori(0, B - 1) as b:
                dve_units(dve, b, 1, nxt=(b + 1, 0, b), prev=(b, 0))
                dve_units(dve, b + 1, 0, nxt=(b + 1, 1, b), prev=(b, 1))
            b = B - 1
            dve_units(dve, b, 1, prev=(b, 0))
            for h in range(2):
                dve_y(dve, NSEQ - 1, 1, h)

        def pool_hc(pool, u, n):
            pool.wait_ge(scan_done, u + 1)
            pool.wait_ge(c_out, 2 * u + 2)
            atleast(pool, hc_used, 2 * (u - 1))
            nc.gpsimd.tensor_tensor(hc[n % 2][:, :], hh[n % 2][:, :], cc[n % 2][:, :], ALU.mult).then_inc(hc_done, 1)

        def pool_dt(pool, q):
            settle(pool, lost_done, q + 1, pool_passed)
            nc.gpsimd.tensor_tensor(rl[:, :], rl[:, :], ex[:, :], ALU.subtract).then_inc(part_done, 1)

        def pool_gate(pool, q, s, b):
            pool.wait_ge(y_free, 2 * q + 2)
            atleast(pool, px_free, use(2 * b + 2, 0, b - 1) + 2 if not isinstance(b, int) or b > 0 else 0)
            nc.gpsimd.tensor_tensor(yg[s][:, :], yt[:, :], gate[s][:, :], ALU.mult).then_inc(yg_done, 1)

        def pool_units(pool, b, s, nxt=None, prev=None):
            q = 2 * b + s
            for n in range(NS):
                pool_hc(pool, NS * q + n, n)
                if prev and n == 2:
                    pool_gate(pool, q - 1, prev[1], prev[0])
                if nxt and n == 8:
                    pool_dt(pool, 2 * nxt[0] + nxt[1])

        @block.gpsimd
        def _(pool):
            pool_dt(pool, 0)
            pool_units(pool, 0, 0, nxt=(0, 1, 0))
            with pool.Fori(0, B - 1) as b:
                pool_units(pool, b, 1, nxt=(b + 1, 0, b), prev=(b, 0))
                pool_units(pool, b + 1, 0, nxt=(b + 1, 1, b), prev=(b, 1))
            pool_units(pool, B - 1, 1, prev=(B - 1, 0))
            pool_gate(pool, NSEQ - 1, 1, B - 1)

        @block.sync
        def _(sp):
            sp.wait_ge(xm_done, 1)
            for r in range(2):
                sp.dma_start(w["xm2"][C * r:C * r + C, :].rearrange("c (p t) -> c p t", p=2),
                             w["xm"][:, :].rearrange("c (p r t) -> c r p t", p=2, r=2)[:, r, :, :]).then_inc(stacked, 16)
            sp.wait_ge(stacked, 32)


class Attention:

    GRP = T2C // 128

    def __init__(self, nc, ctx, w, causal):
        tag = "l1_" if causal else "ex_"

        def sb(name, shape):
            return ctx.enter_context(nc.sbuf_tensor(tag + name, shape, FP32))

        def ps(name, shape):
            return ctx.enter_context(nc.psum_tensor(tag + name, shape, FP32))

        self.nc, self.w, self.causal = nc, w, causal
        self.qt, self.kt = sb("qt", [128, T2C]), sb("kt", [128, T2C])
        self.vv = sb("vv", [128, self.GRP, 2, VW])
        self.qs = [sb(f"qs_{r}", [128, 128]) for r in range(2)]
        self.p = [sb(f"p_{r}", [128, L]) for r in range(2)]
        self.pts = [sb(f"pts_{r}", [128, L]) for r in range(2)]
        self.o2 = sb("o2", [128, 2, C])
        self.mx, self.nm, self.rc = sb("mx", [128, 2]), sb("nm", [128, 2]), sb("rc", [128, 2])
        self.s = [ps(f"s_{r}", [128, L]) for r in range(2)]
        self.pt = [ps(f"pt_{j}", [128, HALF]) for j in range(2)]
        self.ob = [ps(f"ob_{r}", [128, HALF]) for r in range(2)]
        names = ("at_zero", "qk_full", "q_out", "k_out", "v_full", "v_out0", "v_out1", "qs_ready", "s_full", "mx_done",
                 "nm_done", "p_done", "tr0", "tr1", "pt0_out", "pt1_out", "o_full", "rc_done", "o_out", "ot_full", "ot_out")
        self.passed = ctx.enter_context(nc.semaphore(tag + "passed"))
        (self.at_zero, self.qk_full, self.q_out, self.k_out, self.v_full, self.v_out0, self.v_out1, self.qs_ready,
         self.s_full, self.mx_done, self.nm_done, self.p_done, self.tr0, self.tr1, self.pt0_out, self.pt1_out,
         self.o_full, self.rc_done, self.o_out, self.ot_full, self.ot_out) = (
            ctx.enter_context(nc.semaphore(tag + name)) for name in names)

    def before(self, eng, sem, k, g, value):
        if not (isinstance(g, int) and g == 0 and (self.causal is False or value <= 0)):
            atleast(eng, sem, value)

    def blocks(self, i):
        return i + 1 if self.causal else L // 128

    def seconds(self, k, g, i, r):
        if not self.causal:
            return 2 * self.GRP * k + 2 * g + r
        return (g - i) + 2 * (i - 4) + r

    def prepare_pool(self, pool):
        nc = self.nc
        nc.gpsimd.memset(self.vv[:, :, :, :], 1.0).then_inc(self.at_zero, 1)
        for r in range(2):
            nc.gpsimd.memset(self.qs[r][:, :], 0.0).then_inc(self.at_zero, 1)

    def pe_project(self, pe, k, src, src_wait, wq, wk, wv):
        nc = self.nc
        for c in range(4):
            src_wait(pe, c)
            for m, (wt, out) in enumerate(((wq, self.q_out), (wk, self.k_out))):
                atleast(pe, out, 4 * k + c)
                nc.tensor.matmul(self.pt[m][:, :], wt[:, :], src[:, c * HALF:(c + 1) * HALF],
                                 start=True, stop=True).then_inc(self.qk_full, 1)
        for g in range(self.GRP):
            out = (self.v_out0, self.v_out1)[g % 2]
            atleast(pe, out, 8 * k + g // 2)
            nc.tensor.matmul(self.ob[g % 2][:, 0:128], src[:, g * 128:(g + 1) * 128], wv[:, :],
                             start=True, stop=True).then_inc(self.v_full, 1)

    def act_project(self, act, k):
        nc = self.nc
        for c in range(4):
            act.wait_ge(self.qk_full, 8 * k + 2 * c + 1)
            nc.scalar.activation(self.qt[:, c * HALF:(c + 1) * HALF], self.pt[0][:, :], ACT.Copy).then_inc(self.q_out, 1)
        act.wait_ge(self.at_zero, 3)
        for g in range(1, self.GRP, 2):
            act.wait_ge(self.v_full, self.GRP * k + g + 1)
            nc.scalar.activation(self.vv[:, g, :, 0:C], self.ob[1][:, 0:128].rearrange("p (r c) -> p r c", r=2),
                                 ACT.Copy).then_inc(self.v_out1, 1)

    def dve_project(self, dve, k):
        nc = self.nc
        for c in range(4):
            dve.wait_ge(self.qk_full, 8 * k + 2 * c + 2)
            nc.vector.tensor_copy(self.kt[:, c * HALF:(c + 1) * HALF], self.pt[1][:, :]).then_inc(self.k_out, 1)
        dve.wait_ge(self.at_zero, 3)
        for g in range(0, self.GRP, 2):
            dve.wait_ge(self.v_full, self.GRP * k + g + 1)
            nc.vector.tensor_copy(self.vv[:, g, :, 0:C], self.ob[0][:, 0:128].rearrange("p (r c) -> p r c", r=2)).then_inc(self.v_out0, 1)

    def pe_scores(self, pe, k, g, i, p, r):
        nc, t = self.nc, 2 * (self.GRP * k + g) + r
        pe.wait_ge(self.qs_ready, t + 1)
        self.before(pe, self.p_done, k, g, t - 1)
        full = i * 128 if self.causal else L
        parts = [(a, min(HALF, full - a)) for a in range(0, full, HALF)]
        for a, n in parts:
            last = nc.tensor.matmul(self.s[r][:, a:a + n], self.qs[r][:, :], self.kt[:, bass.ds(p * L + a, n)],
                                    start=True, stop=True)
        if self.causal:
            nc.tensor.matmul(self.s[r][:, full:full + 128], self.qs[r][:, :], self.kt[:, bass.ds(p * L + full, 128)],
                             start=True, stop=False)
            last = nc.tensor.matmul(self.s[r][:, full:full + 128], self.w["cst"][:, IDN:IDN + 128],
                                    self.w["cst"][:, CAUS:CAUS + 128], start=False, stop=True)
        last.then_inc(self.s_full, 1)

    def pe_turn(self, pe, k, g, i, r):
        nc, t, n = self.nc, 2 * (self.GRP * k + g) + r, self.blocks(i)
        pe.wait_ge(self.p_done, t + 1)
        if isinstance(k, int) and isinstance(g, int) and k == 0 and g == 0 and r == 0:
            pe.wait_ge(self.k_out, 4)
        for j in range(min(n, 4)):
            if j == 0:
                atleast(pe, self.pt0_out, t)
            last = nc.tensor.transpose(self.pt[0][:, j * 128:(j + 1) * 128], self.p[r][:, j * 128:(j + 1) * 128],
                                       self.w["cst"][:, IDN:IDN + 128])
        last.then_inc(self.tr0, 1)
        for j in range(4, n):
            if j == 4:
                atleast(pe, self.pt1_out, self.seconds(k, g, i, r))
            last = nc.tensor.transpose(self.pt[1][:, (j - 4) * 128:(j - 3) * 128], self.p[r][:, j * 128:(j + 1) * 128],
                                       self.w["cst"][:, IDN:IDN + 128])
        if n > 4:
            last.then_inc(self.tr1, 1)

    def pe_values(self, pe, k, g, i, p, r):
        nc, t, n = self.nc, 2 * (self.GRP * k + g) + r, self.blocks(i)
        pe.wait_ge(self.pt0_out, t + 1)
        if n > 4:
            pe.wait_ge(self.pt1_out, self.seconds(k, g, i, r) + 1)
        self.before(pe, self.o_out, k, g, t - 1)
        for j in range(n):
            last = nc.tensor.matmul(self.ob[r][:, 0:VW], self.pts[r][:, j * 128:(j + 1) * 128],
                                    self.vv[:, bass.ds(p * 8 + j, 1), r, :].rearrange("p a c -> p (a c)"),
                                    start=(j == 0), stop=(j == n - 1))
        last.then_inc(self.o_full, 1)

    def pe_back(self, pe, k, g):
        nc, n = self.nc, self.GRP * k + g
        pe.wait_ge(self.o_out, 2 * n + 2)
        atleast(pe, self.ot_out, n)
        nc.tensor.transpose(self.ob[1][:, 256:384], self.o2[:, :, :].rearrange("p r c -> p (r c)"),
                            self.w["cst"][:, IDN:IDN + 128]).then_inc(self.ot_full, 1)

    def pe_group(self, pe, k, g, i, p, prev):
        for r in range(2):
            self.pe_scores(pe, k, g, i, p, r)
            if prev:
                self.pe_values(pe, k, prev[0], prev[1], prev[2], r)
            if r == 0 and prev:
                self.pe_turn(pe, k, prev[0], prev[1], 1)
            if r == 1:
                self.pe_turn(pe, k, g, i, 0)
        if prev:
            self.pe_back(pe, k, prev[0])

    def pe_tail(self, pe, k, g, i, p):
        self.pe_values(pe, k, g, i, p, 0)
        self.pe_turn(pe, k, g, i, 1)
        self.pe_values(pe, k, g, i, p, 1)
        self.pe_back(pe, k, g)

    def dve_max(self, dve, k, g, i, r):
        nc, t = self.nc, 2 * (self.GRP * k + g) + r
        dve.wait_ge(self.s_full, t + 1)
        self.before(dve, self.nm_done, k, g, t - 1)
        nc.vector.reduce_max(self.mx[:, r:r + 1], self.s[r][:, 0:128 * self.blocks(i)], AX.X).then_inc(self.mx_done, 1)
        dve.wait_ge(self.mx_done, t + 1)
        self.before(dve, self.p_done, k, g, t - 1)
        nc.vector.tensor_scalar(self.nm[:, r:r + 1], self.mx[:, r:r + 1], -SCALE, None, ALU.mult).then_inc(self.nm_done, 1)

    def dve_turned(self, dve, k, g, i, r):
        nc, t = self.nc, 2 * (self.GRP * k + g) + r
        n = 128 * min(self.blocks(i), 4)
        dve.wait_ge(self.tr0, t + 1)
        self.before(dve, self.o_full, k, g, t - 1)
        nc.vector.tensor_copy(self.pts[r][:, 0:n], self.pt[0][:, 0:n]).then_inc(self.pt0_out, 1)

    def dve_output(self, dve, k, g, r):
        nc, t = self.nc, 2 * (self.GRP * k + g) + r
        dve.wait_ge(self.o_full, t + 1)
        self.before(dve, self.o_out, k, g, t - 1)
        nc.vector.reciprocal(self.rc[:, r:r + 1], self.ob[r][:, C:C + 1]).then_inc(self.rc_done, 1)
        dve.wait_ge(self.rc_done, t + 1)
        if r == 0:
            atleast(dve, self.ot_full, self.GRP * k + g)
        nc.vector.tensor_scalar(self.o2[:, r, :], self.ob[r][:, 0:C], self.rc[:, r:r + 1], None, ALU.mult).then_inc(self.o_out, 1)

    def dve_group(self, dve, k, g, i, prev, finish):
        for r in range(2):
            self.dve_max(dve, k, g, i, r)
            if prev:
                self.dve_output(dve, k, prev[0], r)
            if r == 0 and prev:
                self.dve_turned(dve, k, prev[0], prev[1], 1)
            if r == 1:
                self.dve_turned(dve, k, g, i, 0)
        if prev:
            finish(dve, k, prev[0])

    def dve_tail(self, dve, k, g, i, finish):
        self.dve_output(dve, k, g, 0)
        self.dve_turned(dve, k, g, i, 1)
        self.dve_output(dve, k, g, 1)
        finish(dve, k, g)

    def act_exp(self, act, k, g, i, r):
        nc, t, n = self.nc, 2 * (self.GRP * k + g) + r, 128 * self.blocks(i)
        act.wait_ge(self.nm_done, t + 1)
        self.before(act, self.tr0, k, g, t - 1)
        if not self.causal:
            self.before(act, self.tr1, k, g, t - 1)
        elif i > 4:
            act.wait_ge(self.tr1, self.seconds(k, g, i, r) - 1)
        nc.scalar.activation(self.p[r][:, 0:n], self.s[r][:, 0:n], ACT.Exp, bias=self.nm[:, r:r + 1],
                             scale=SCALE).then_inc(self.p_done, 1)

    def act_turned(self, act, k, g, i, r):
        nc, t = self.nc, 2 * (self.GRP * k + g) + r
        n = 128 * (self.blocks(i) - 4)
        if n <= 0:
            return
        act.wait_ge(self.tr1, self.seconds(k, g, i, r) + 1)
        self.before(act, self.o_full, k, g, t - 1)
        nc.scalar.activation(self.pts[r][:, HALF:HALF + n], self.pt[1][:, 0:n], ACT.Copy).then_inc(self.pt1_out, 1)

    def act_group(self, act, k, g, i, prev):
        self.act_exp(act, k, g, i, 0)
        if prev:
            self.act_turned(act, k, prev[0], prev[1], 1)
        self.act_exp(act, k, g, i, 1)
        self.act_turned(act, k, g, i, 0)

    def pool_group(self, pool, k, g):
        nc = self.nc
        for r in range(2):
            t = 2 * (self.GRP * k + g) + r
            self.before(pool, self.s_full, k, g, t - 1)
            if not (isinstance(t, int) and t == 0):
                settle(pool, self.qs_ready, t, self.passed)
            rows = slice(C * r, C * r + C)
            nc.gpsimd.tensor_copy(self.qs[r][rows, :], self.qt[rows, bass.ds(g * 128, 128)]).then_inc(self.qs_ready, 1)

    def each(self, eng, group, tail):
        half = self.GRP // 2
        if self.causal:
            prev = None
            for p in range(2):
                for i in range(half):
                    group(p * half + i, i, p, prev)
                    prev = (p * half + i, i, p)
            tail(*prev)
            return
        group(0, 0, 0, None)
        group(1, 0, 0, (0, 0, 0))
        with eng.Fori(2, half) as g:
            group(g, 0, 0, (g - 1, 0, 0))
        group(half, 0, 1, (half - 1, 0, 0))
        with eng.Fori(half + 1, 2 * half) as g:
            group(g, 0, 1, (g - 1, 0, 1))
        tail(self.GRP - 1, 0, 1)

    def pe_all(self, pe, k):
        if isinstance(k, int):
            pe.wait_ge(self.at_zero, 3)
        pe.wait_ge(self.k_out, 4 * k + 4)
        pe.wait_ge(self.v_out0, 8 * k + 8)
        pe.wait_ge(self.v_out1, 8 * k + 8)
        self.each(pe, lambda g, i, p, prev: self.pe_group(pe, k, g, i, p, prev), lambda g, i, p: self.pe_tail(pe, k, g, i, p))

    def act_all(self, act, k):
        self.each(act, lambda g, i, p, prev: self.act_group(act, k, g, i, prev), lambda g, i, p: self.act_turned(act, k, g, i, 1))

    def dve_all(self, dve, k, finish):
        self.each(dve, lambda g, i, p, prev: self.dve_group(dve, k, g, i, prev, finish),
                  lambda g, i, p: self.dve_tail(dve, k, g, i, finish))

    def pool_all(self, pool, k):
        pool.wait_ge(self.q_out, 4 * k + 4)
        self.pool_group(pool, k, 0)
        with pool.Fori(1, self.GRP) as g:
            self.pool_group(pool, k, g)


def build_attend(nc, w, inp):
    ctx = ExitStack()
    with ctx:
        def sb(name, shape):
            return ctx.enter_context(nc.sbuf_tensor(name, shape, FP32))

        def sem(name):
            return ctx.enter_context(nc.semaphore(name))

        at = Attention(nc, ctx, w, causal=True)
        za, t1, zq = sb("za", [128, T2C]), sb("t1", [128, T2C]), sb("zq", [128, T2C])
        sq, sd = sb("lsq", [128, T2C]), sb("lsd", [128, T2C])
        ln_dev, ln_sq, ln_var, ln_sd, ln_rs, ln_z = (sem("ln_dev"), sem("ln_sq"), sem("ln_var"), sem("ln_sd"), sem("ln_rs"), sem("ln_z"))
        zb_done, wp_full, t1_done, t2_done = sem("zb_done"), sem("wp_full"), sem("t1_done"), sem("t2_done")
        NCH = T2C // HALF

        def col(c):
            return slice(c * HALF, (c + 1) * HALF)

        dev_at = [at.s[0][:, 0:HALF], at.s[0][:, HALF:L], at.ob[0][:, :], at.ob[1][:, :]]
        var_at = [at.s[1][:, 0:HALF], at.s[1][:, HALF:L], at.pt[0][:, :], at.pt[1][:, :]]

        def pe_norm(pe, call, src, ready):
            for c in range(NCH):
                ready(pe, c)
                nc.tensor.matmul(dev_at[c], w["cst"][:, CEN:CEN + 128], src[:, col(c)],
                                 start=True, stop=True).then_inc(ln_dev, 1)
            for c in range(NCH):
                pe.wait_ge(ln_sq, NCH * call + c + 1)
                nc.tensor.matmul(var_at[c], w["cst"][:, MEAN:MEAN + 128], sq[:, col(c)],
                                 start=True, stop=True).then_inc(ln_var, 1)

        def act_norm(act, call):
            for c in range(NCH):
                act.wait_ge(ln_dev, NCH * call + c + 1)
                nc.scalar.activation(sq[:, col(c)], dev_at[c], ACT.Square).then_inc(ln_sq, 1)
            for c in range(NCH):
                act.wait_ge(ln_var, NCH * call + c + 1)
                nc.scalar.activation(sd[:, col(c)], var_at[c], ACT.Ln, bias=w["eps"][:, :]).then_inc(ln_sd, 1)
            for c in range(NCH):
                act.wait_ge(ln_sd, NCH * call + c + 1)
                nc.scalar.activation(sd[:, col(c)], sd[:, col(c)], ACT.Exp, scale=-0.5).then_inc(ln_rs, 1)

        def dve_norm(dve, call, dst, then=None):
            for c in range(NCH):
                n = NCH * call + c
                dve.wait_ge(ln_rs, n + 1)
                nc.vector.tensor_tensor(dst[:, col(c)], dev_at[c], sd[:, col(c)], ALU.mult).then_inc(ln_z, 1)
                if then:
                    then(c, n)

        block = ctx.enter_context(nc.Block())

        @block.gpsimd
        def _(pool):
            at.prepare_pool(pool)
            pool.wait_ge(at.at_zero, 3)
            at.pool_all(pool, 0)

        @block.tensor
        def _(pe):
            pe_norm(pe, 0, w["xm2"], lambda eng, c: None)
            for c in range(NCH):
                pe.wait_ge(zb_done, c + 1)
                atleast(pe, t1_done, c - 1)
                nc.tensor.matmul(at.pt[c % 2][:, :], w["wp"][:, :], za[:, col(c)], start=True, stop=True).then_inc(wp_full, 1)
            pe_norm(pe, 1, t1, lambda eng, c: eng.wait_ge(t1_done, c + 1))
            at.pe_project(pe, 0, zq, lambda eng, c: eng.wait_ge(ln_z, NCH + c + 1), w["wq1"], w["wk1"], w["wv1"])
            at.pe_all(pe, 0)
            pe_norm(pe, 2, w["t2"], lambda eng, c: eng.wait_ge(at.ot_out, at.GRP))

        @block.scalar
        def _(act):
            act_norm(act, 0)
            act_norm(act, 1)
            at.act_project(act, 0)
            at.act_all(act, 0)
            act_norm(act, 2)

        @block.vector
        def _(dve):
            def affine(c, n):
                dve.wait_ge(ln_z, n + 1)
                nc.vector.tensor_scalar(za[:, col(c)], za[:, col(c)], w["gam"][:, :], w["bet"][:, :],
                                        ALU.mult, ALU.add).then_inc(zb_done, 1)

            dve_norm(dve, 0, za, affine)
            for c in range(NCH):
                dve.wait_ge(wp_full, c + 1)
                nc.vector.scalar_tensor_tensor(t1[:, col(c)], at.pt[c % 2][:, :], w["bp"][:, :], w["xst"][:, col(c)],
                                               ALU.add, ALU.add).then_inc(t1_done, 1)
            dve_norm(dve, 1, zq)
            at.dve_project(dve, 0)

            def finish(eng, k, g):
                eng.wait_ge(at.ot_full, g + 1)
                nc.vector.tensor_tensor(w["t2"][:, bass.ds(g * 128, 128)], at.ob[1][:, 256:384], t1[:, bass.ds(g * 128, 128)],
                                        ALU.add).then_inc(at.ot_out, 1)

            at.dve_all(dve, 0, finish)
            dve_norm(dve, 2, w["h"])


def build_experts(nc, w, inp, out):
    ctx = ExitStack()
    with ctx:
        def sb(name, shape, dt=FP32):
            return ctx.enter_context(nc.sbuf_tensor(name, shape, dt))

        def sem(name):
            return ctx.enter_context(nc.semaphore(name))

        at = Attention(nc, ctx, w, causal=False)
        h, yy = w["h"], sb("yy", [128, T2C])
        wa = [sb(f"wa_{i}", [128, 128]) for i in range(4)]
        w1 = [sb(f"w1_{r}", [128, HID]) for r in range(2)]
        w2 = [sb(f"w2_{r}", [128, 2, 128]) for r in range(2)]
        b1, b2 = sb("b1", [128, 2]), sb("b2", [128, 1])
        zh = [[sb(f"zh_{r}{m}", [128, HALF]) for m in range(2)] for r in range(2)]
        row, top, idx = sb("row", [1, 32]), sb("top", [1, 8]), sb("idx", [1, 8], U32)
        nxt, nxt_i = sb("nxt", [1, 1]), sb("nxt_i", [1, 1], I32)
        word = sb("word", [1, 4], I32)

        zeroed, att_loaded, ffn_loaded = sem("ex_zeroed"), sem("att_loaded"), sem("ffn_loaded")
        row_full, pick, word_done, word_read = sem("row_full"), sem("pick"), sem("word_done"), sem("word_read")
        wo_full, h_att, z1_full, zh_act, zh_dve, z2_full, h_ffn = (
            sem("wo_full"), sem("h_att"), sem("z1_full"), sem("zh_act"), sem("zh_dve"), sem("z2_full"), sem("h_ffn"))
        added, stored, passed = sem("added"), sem("stored"), sem("passed")
        NCH, GRP = T2C // HALF, Attention.GRP
        ATT_LOADS, FFN_LOADS = 8 * 16, 8 * 16
        RUN = 11
        PICK = 9

        def col(c):
            return slice(c * HALF, (c + 1) * HALF)

        def run(eng, attend, feed, select=None):
            word_regs = [eng.alloc_register(f"word{i}") for i in range(4)]
            n_steps, n_att, n_ffn = (eng.alloc_register(name) for name in ("n_steps", "n_att", "n_ffn"))
            for reg in (n_steps, n_att, n_ffn):
                eng.reg_mov(reg, 0)
            eng.wait_ge(word_done, 1)
            eng.reg_load(word_regs, word[0:1, 0:4]).then_inc(word_read, 1)
            def step(b):
                with eng.If(eng.snap(word_regs[0]) == b):
                    e = b * NOPS + eng.snap(word_regs[3], min_val=0, max_val=NOPS - 1)
                    with eng.If(eng.snap(word_regs[1]) > 0):
                        attend(eng.snap(n_att), e)
                        eng.reg_add(n_att, n_att, 1)
                    with eng.If(eng.snap(word_regs[2]) > 0):
                        feed(eng.snap(n_ffn), eng.snap(n_att), e)
                        eng.reg_add(n_ffn, n_ffn, 1)
                    if select:
                        select(eng.snap(n_steps) + 1, eng.snap(n_att), eng.snap(n_ffn), b)
                    settle(eng, word_done, eng.snap(n_steps) + 2, passed)
                    eng.reg_add(n_steps, n_steps, 1)
                    eng.reg_load(word_regs, word[0:1, 0:4]).then_inc(word_read, 1)

            with eng.Fori(0, NSTEP // RUN) as j:
                with eng.If(eng.snap(word_regs[0]) < (j + 1) * RUN):
                    with eng.Fori(0, RUN) as i:
                        step(j * RUN + i)

        block = ctx.enter_context(nc.Block())

        @block.sync
        def _(sp):
            def attend(k, e):
                for i, name in enumerate(("wq", "wk", "wv", "wo")):
                    src = inp[name].rearrange("b o i j -> i (b o) j")[:, bass.ds(e, 1), :].rearrange("i a j -> i (a j)")
                    for r in range(2):
                        s = slice(C * r, C * r + C)
                        sp.dma_start(wa[i][s, s], src).then_inc(att_loaded, 16)

            def feed(k, ka, e):
                s1 = inp["ffn_w1"].rearrange("b o i j -> i (b o) j")[:, bass.ds(e, 1), :].rearrange("i a j -> i (a j)")
                s2 = inp["ffn_w2"].rearrange("b o (m i) j -> i (b o) m j", m=2)[:, bass.ds(e, 1), :, :].rearrange("i a m j -> i (a m) j")
                sb1 = inp["ffn_b1"].rearrange("b o (m i) -> i m (b o)", m=2)
                sb2 = inp["ffn_b2"].rearrange("b o i -> i (b o)")[:, bass.ds(e, 1)]
                for r in range(2):
                    s = slice(C * r, C * r + C)
                    sp.dma_start(w1[r][s, :], s1).then_inc(ffn_loaded, 16)
                    sp.dma_start(w2[r][:, :, s], s2).then_inc(ffn_loaded, 16)
                    sp.dma_start(b2[s, :], sb2).then_inc(ffn_loaded, 16)
                for m in range(2):
                    sp.dma_start(b1[:, m:m + 1], sb1[:, m, bass.ds(e, 1)]).then_inc(ffn_loaded, 16)

            sp.wait_ge(zeroed, 8)
            run(sp, attend, feed)
            dst = out.rearrange("(p r) c h w -> r c p (h w)", r=2)
            for c in range(NCH):
                sp.wait_ge(added, c + 1)
                p, a = c // 2, (c % 2) * HALF
                for r in range(2):
                    sp.dma_start(dst[r, :, p, a:a + HALF], yy[C * r:C * r + C, col(c)]).then_inc(stored, 16)
            sp.wait_ge(stored, 2 * NCH * 16)

        @block.gpsimd
        def _(pool):
            for t in wa:
                nc.gpsimd.memset(t[:, :], 0.0).then_inc(zeroed, 1)
            for t in w1:
                nc.gpsimd.memset(t[:, :], 0.0).then_inc(zeroed, 1)
            for t in w2:
                nc.gpsimd.memset(t[:, :, :], 0.0).then_inc(zeroed, 1)
            at.prepare_pool(pool)
            pool.wait_ge(at.at_zero, 3)
            run(pool, lambda k, e: at.pool_all(pool, k), lambda k, ka, e: None)

        @block.tensor
        def _(pe):
            def attend(k, e):
                pe.wait_ge(att_loaded, ATT_LOADS * k + ATT_LOADS)
                at.pe_project(pe, k, h, lambda eng, c: None, wa[0], wa[1], wa[2])
                at.pe_all(pe, k)
                for c in range(NCH):
                    pe.wait_ge(at.ot_out, GRP * k + 4 * c + 4)
                    if c >= 2:
                        pe.wait_ge(h_att, NCH * k + c - 1)
                    nc.tensor.matmul(at.pt[c % 2][:, :], wa[3][:, :], yy[:, col(c)], start=True, stop=True).then_inc(wo_full, 1)

            def hidden(k, c):
                for r in range(2):
                    for m, used in ((0, zh_act), (1, zh_dve)):
                        if c:
                            pe.wait_ge(used, 2 * (NCH * k + c - 1) + r + 1)
                        nc.tensor.matmul(at.s[r][:, col(m)], w1[r][:, 128 * m:128 * m + 128], h[:, col(c)],
                                         start=True, stop=True).then_inc(z1_full, 1)

            def feed(k, ka, e):
                pe.wait_ge(ffn_loaded, FFN_LOADS * k + FFN_LOADS)
                pe.wait_ge(h_att, NCH * ka)
                hidden(k, 0)
                for c in range(NCH):
                    if c + 1 < NCH:
                        hidden(k, c + 1)
                    pe.wait_ge(zh_act, 2 * (NCH * k + c) + 2)
                    pe.wait_ge(zh_dve, 2 * (NCH * k + c) + 2)
                    if c >= 2:
                        pe.wait_ge(h_ffn, NCH * k + c - 1)
                    for n, (r, m) in enumerate(((0, 0), (0, 1), (1, 0), (1, 1))):
                        last = nc.tensor.matmul(at.pt[c % 2][:, :], w2[r][:, m, :], zh[r][m][:, :],
                                                start=(n == 0), stop=(n == 3))
                    last.then_inc(z2_full, 1)

            def turn_row():
                nc.tensor.transpose(at.ob[0][:, 0:128], h[:, 0:128], w["cst"][:, IDN:IDN + 128]).then_inc(row_full, 1)

            def select(j, ka, kf, b):
                pe.wait_ge(h_att, NCH * ka)
                pe.wait_ge(h_ffn, NCH * kf)
                turn_row()

            pe.wait_ge(at.at_zero, 3)
            turn_row()
            run(pe, attend, feed, select)

        @block.scalar
        def _(act):
            def attend(k, e):
                at.act_project(act, k)
                at.act_all(act, k)

            def feed(k, ka, e):
                for c in range(NCH):
                    for r in range(2):
                        act.wait_ge(z1_full, 4 * (NCH * k + c) + 2 * r + 1)
                        if r == 0:
                            act.wait_ge(z2_full, NCH * k + c)
                        nc.scalar.activation(zh[r][0][:, :], at.s[r][:, col(0)], ACT.Relu, bias=b1[:, 0:1]).then_inc(zh_act, 1)

            run(act, attend, feed)

        @block.vector
        def _(dve):
            def finish(eng, k, g):
                n = GRP * k + g
                eng.wait_ge(at.ot_full, n + 1)
                nc.vector.tensor_scalar(yy[:, bass.ds(g * 128, 128)], at.ob[1][:, 256:384], 1.0, None, ALU.mult).then_inc(at.ot_out, 1)

            def attend(k, e):
                at.dve_project(dve, k)
                at.dve_all(dve, k, finish)
                for c in range(NCH):
                    dve.wait_ge(wo_full, NCH * k + c + 1)
                    nc.vector.tensor_copy(h[:, col(c)], at.pt[c % 2][:, :]).then_inc(h_att, 1)

            def feed(k, ka, e):
                for c in range(NCH):
                    for r in range(2):
                        dve.wait_ge(z1_full, 4 * (NCH * k + c) + 2 * r + 2)
                        if r == 0:
                            dve.wait_ge(z2_full, NCH * k + c)
                        nc.vector.tensor_scalar(zh[r][1][:, :], at.s[r][:, col(1)], b1[:, 1:2], 0.0, ALU.add, ALU.max).then_inc(zh_dve, 1)
                    dve.wait_ge(z2_full, NCH * k + c + 1)
                    nc.vector.tensor_scalar(h[:, col(c)], at.pt[c % 2][:, :], b2[:, :], None, ALU.add).then_inc(h_ffn, 1)

            def select(j, ka, kf, b):
                base = PICK * j
                dve.wait_ge(row_full, j + 1)
                nc.vector.tensor_copy(row[:, 0:NOPS], at.ob[0][0:1, 0:NOPS]).then_inc(pick, 1)
                settle(dve, pick, base + 1, passed)
                nc.vector.max(top[:, :], row[:, 0:NOPS]).then_inc(pick, 1)
                settle(dve, pick, base + 2, passed)
                nc.vector.max_index(idx[:, :], top[:, :], row[:, 0:NOPS]).then_inc(pick, 1)
                settle(dve, pick, base + 3, passed)
                op = dve.value_load(idx[0:1, 0:1], min_val=0, max_val=NOPS - 1)
                at_step = (b + 1) * NOPS + op
                nc.vector.tensor_reduce(nxt[:, :], w["code"][0:1, bass.DynSlice(at_step, NSTEP, NOPS)], AX.X, ALU.min).then_inc(pick, 1)
                dve.wait_ge(pick, base + 4)
                nc.vector.tensor_copy(nxt_i[:, :], nxt[:, :]).then_inc(pick, 1)
                dve.wait_ge(pick, base + 5)
                atleast(dve, word_read, 5 * j)
                nc.vector.tensor_scalar(word[:, 0:1], nxt_i[:, :], 2, None, ALU.arith_shift_right).then_inc(pick, 1)
                nc.vector.tensor_scalar(word[:, 1:2], nxt_i[:, :], 1, None, ALU.bitwise_and).then_inc(pick, 1)
                nc.vector.tensor_scalar(word[:, 2:3], nxt_i[:, :], 1, 1, ALU.arith_shift_right, ALU.bitwise_and).then_inc(pick, 1)
                nc.vector.tensor_copy(word[:, 3:4], idx[:, 0:1]).then_inc(pick, 1)
                dve.wait_ge(pick, base + PICK)
                dve.sem_inc(word_done, 1)

            select(0, 0, 0, -1)
            run(dve, attend, feed, select)
            for c in range(NCH):
                nc.vector.tensor_tensor(yy[:, col(c)], w["t2"][:, col(c)], h[:, col(c)], ALU.add).then_inc(added, 1)


INPUTS = {"x": "x", "gamma": "L0_conv_gamma", "beta": "L0_conv_beta", "W_in": "L0_conv_W_in",
          "conv_w": "L0_conv_conv_w", "conv_b": "L0_conv_conv_b", "W_x": "L0_conv_W_x", "W_dt": "L0_conv_W_dt",
          "b_dt": "L0_conv_b_dt", "A_log": "L0_conv_A_log", "D_skip": "L0_conv_D_skip", "W_out": "L0_conv_W_out",
          "W_p": "L0_conv_W_p", "b_p": "L0_conv_b_p", "s1": "L0_conv_s1", "s2": "L0_conv_s2",
          "Wq": "L1_attn_Wq", "Wk": "L1_attn_Wk", "Wv": "L1_attn_Wv",
          "ffn_w1": "L1_ffn_ffn_w1", "ffn_b1": "L1_ffn_ffn_b1", "ffn_w2": "L1_ffn_ffn_w2", "ffn_b2": "L1_ffn_ffn_b2",
          "wq": "L1_ffn_wq", "wk": "L1_ffn_wk", "wv": "L1_ffn_wv", "wo": "L1_ffn_wo",
          "attn_mask": "L1_ffn_attn_mask", "ffn_mask": "L1_ffn_ffn_mask"}


def program(nc, inp, out):
    ctx = ExitStack()
    with ctx:
        shapes = {"cst": [128, CONSTW], "xst": [128, T2C], "gam": [128, 1], "bet": [128, 1], "bp": [128, 1],
                  "eps": [128, 1], "wp": [128, 128], "wq1": [128, 128], "wk1": [128, 128], "wv1": [128, 128],
                  "xm2": [128, T2C], "code": [1, 2 * NSTEP * NOPS + NOPS]}
        scan_only = {"xs": [128, NSEQ * XW], "cb": [128, 1], "hcb": [128, 1], "bdt": [128, 1], "dsk": [128, 1],
                     "scol": [128, 2], "aneg": [128, NS], "wca": [128, 128], "wcb": [128, 128], "wg": [128, 128],
                     "wbc": [128, 128], "wdt": [128, 128], "wo": [128, 128], "res": [128, 2, 128]}
        w = {name: ctx.enter_context(nc.sbuf_tensor("w_" + name, shape, FP32)) for name, shape in shapes.items()}
        with ExitStack() as scans:
            for name, shape in scan_only.items():
                w[name] = scans.enter_context(nc.sbuf_tensor("w_" + name, shape, FP32))
            w["sel"] = scans.enter_context(nc.sbuf_tensor("w_sel", [128, 32, 128], BF16))
            build_prepare(nc, w, inp)
            with nc.sbuf_tensor("w_xm", [C, B * L], FP32) as w["xm"]:
                build_scan(nc, w, inp)
        w["t2"] = ctx.enter_context(nc.sbuf_tensor("w_t2", [128, T2C], FP32))
        w["h"] = ctx.enter_context(nc.sbuf_tensor("w_h", [128, T2C], FP32))
        build_attend(nc, w, inp)
        build_experts(nc, w, inp, out)


def constants():
    import numpy as np

    t = np.zeros((128, CONSTW), np.float32)
    r = np.arange(128)
    t[:, IDN:IDN + 128] = np.eye(128)
    chan = np.concatenate([np.arange(C), C + (np.arange(C) % 8) * 8 + np.arange(C) // 8])
    t[:, PAIR:PAIR + 128] = 0.5 * (chan[:, None] // 2 == chan[None, :] // 2)
    same = (r[:, None] // C == r[None, :] // C)
    t[:, MEAN:MEAN + 128] = same / C
    t[:, CEN:CEN + 128] = np.eye(128) - same / C
    t[:, CAUS:CAUS + 128] = np.where(r[None, :] <= r[:, None], 0.0, -1e30)
    for part in (0, 64, 96):
        t[part:part + 32, SELV:SELV + 32] = np.eye(32)
    t[:, IOTA:IOTA + 72] = 4 * np.arange(72)
    return t


def kernel(**inputs):
    import numpy as np
    import concourse.bacc as bacc
    from concourse.bass_utils import run_bass_kernel_spmd

    nc = bacc.Bacc("TRN2", target_bir_lowering=False, num_devices=1)
    arrays, inp = {}, {}
    for name, given in INPUTS.items():
        a = np.ascontiguousarray(inputs[given])
        if a.dtype == np.bool_:
            a = np.concatenate([a.reshape(-1), np.zeros(4 * MASKW - a.size, np.bool_)]).view(np.int32)
        arrays["in_" + name] = a
    arrays["in_consts"] = constants()
    for name, a in arrays.items():
        inp[name[3:]] = nc.dram_tensor(name, a.shape, mybir.dt.from_np(a.dtype), kind="ExternalInput").ap()
    out = nc.dram_tensor("out", (B, C, 32, 32), FP32, kind="ExternalOutput").ap()
    program(nc, inp, out)
    r = run_bass_kernel_spmd(nc, [arrays], core_ids=[0])
    return r.results[0]["out"]
```

```python
import concourse.bass as bass
from concourse import mybir
from contextlib import ExitStack

FP32 = mybir.dt.float32
BF16 = mybir.dt.bfloat16
I32 = mybir.dt.int32
U32 = mybir.dt.uint32
U8 = mybir.dt.uint8
ALU = mybir.AluOpType
ACT = mybir.ActivationFunctionType
AX = mybir.AxisListType

B, C, L = 4, 64, 1024
DI, NS, DR = 128, 16, 4
NSEQ = 2 * B
NSTEP, NOPS, HID = 33, 19, 256
XW = L + 4
HALF = 512
T2C = 2 * L
VW = 66
EPS = 1e-5
SCALE = float(C) ** -0.5
IDN, PAIR, CEN, MEAN, CAUS, SELV, IOTA = 0, 128, 256, 384, 512, 640, 672
CONSTW = IOTA + 72
MASKW = -(-NSTEP * NOPS // 4)


def atleast(eng, sem, value):
    if not isinstance(value, int) or value > 0:
        eng.wait_ge(sem, value)


def settle(eng, sem, value, passed):
    eng.wait_ge(sem, value)
    eng.sem_inc(passed, 1)


def build_prepare(nc, w, inp):
    ctx = ExitStack()
    with ctx:
        def sb(name, shape, dt=FP32):
            return ctx.enter_context(nc.sbuf_tensor(name, shape, dt))

        def sem(name):
            return ctx.enter_context(nc.semaphore(name))

        xx = sb("xx", [128, B * L])
        win = sb("win", [128, 2, C])
        conv_w = sb("conv_w", [128, 4])
        nat = sb("nat", [128, 11, 128])
        NCA, NCB, NG, NBC, NDT, NO, NP, NQ, NK, NV, NX = range(11)
        wdtT = sb("wdtT", [128, 128])
        wpT, wpg = sb("wpT", [128, 128]), sb("wpg", [128, 128])
        a_log = sb("a_log", [128, NS])
        stats = sb("stats", [128, B, 2, 6])
        mv = sb("mv", [128, B, 2])
        gstat = sb("gstat", [128, 2, B])
        gdev = sb("gdev", [128, B])
        grs = sb("grs", [128, B])
        z0 = [sb(f"z0_{i}", [128, L]) for i in range(2)]
        sq = [sb(f"sq_{i}", [128, L]) for i in range(2)]
        zt = [sb(f"zt_{b}", [128, L]) for b in range(B)]
        sd = [sb(f"sd_{b}", [128, L]) for b in range(B)]
        pw = [ctx.enter_context(nc.psum_tensor(f"pw{i}", [128, HALF], FP32)) for i in range(2)]
        pg = pw[0]
        pd = [ctx.enter_context(nc.psum_tensor(f"pd_{i}", [128, L], FP32)) for i in range(2)]
        pv = ctx.enter_context(nc.psum_tensor("pv", [128, L], FP32))

        zeroed, x_in, w_in, act_w_in = sem("zeroed"), sem("x_in"), sem("w_in"), sem("act_w_in")
        wpg_done, wp_centred = sem("wpg_done"), sem("wp_centred")
        cst_in, xst_in, dev_out, pool_w_in = sem("cst_in"), sem("xst_in"), sem("dev_out"), sem("pool_w_in")
        scaled, turned, weight_out = sem("scaled"), sem("turned"), sem("weight_out")
        a_exp, stats_done, aggr_done, pair_done = sem("a_exp"), sem("stats_done"), sem("aggr_done"), sem("pair_done")
        gn_chain, gsd_done, grs_done = sem("gn_chain"), sem("gsd_done"), sem("grs_done")
        z0_done, dev_done, sq_done, var_done = sem("z0_done"), sem("dev_done"), sem("sq_done"), sem("var_done")
        sd_done, rs_done, zt_done, dve_x, act_x = sem("sd_done"), sem("rs_done"), sem("zt_done"), sem("dve_x"), sem("act_x")
        sel_done, code_chain = sem("sel_done"), sem("code_chain")
        mask_words = sb("mask_words", [1, 2, MASKW], I32)
        mask_bytes = mask_words[:, :, :].bitcast(U8)
        flags = sb("flags", [1, 2, NSTEP * NOPS])

        cst = w["cst"]
        block = ctx.enter_context(nc.Block())

        @block.sync
        def _(sp):
            xd = inp["x"].rearrange("b c h w -> c b (h w)")
            sp.dma_start(xx[0:C, :].rearrange("c (b t) -> c b t", b=B), xd).then_inc(x_in, 16)
            xg = inp["x"].rearrange("b (g j) h w -> j g b (h w)", j=8)
            for j in range(8):
                sp.dma_start(xx[C + 8 * j:C + 8 * j + 8, :].rearrange("g (b t) -> g b t", b=B),
                             xg[j, :, :, :]).then_inc(x_in, 16)
            sp.dma_start(win[:, :, :], inp["W_in"].rearrange("(j d) c -> d j c", j=2)).then_inc(w_in, 16)
            sp.dma_start(conv_w[:, :], inp["conv_w"].rearrange("d a k -> d (a k)")).then_inc(w_in, 16)
            for half in range(2):
                sp.dma_start(w["gam"][C * half:C * half + C, :], inp["gamma"].rearrange("(c a) -> c a", a=1)).then_inc(w_in, 16)
                sp.dma_start(w["bet"][C * half:C * half + C, :], inp["beta"].rearrange("(c a) -> c a", a=1)).then_inc(w_in, 16)
            for r in range(2):
                sp.dma_start(w["xst"][C * r:C * r + C, :].rearrange("c (p t) -> c p t", p=2),
                             inp["x"].rearrange("(p r) c h w -> r c p (h w)", r=2)[r, :, :, :]).then_inc(xst_in, 16)
            sp.wait_ge(xst_in, 32)

        @block.gpsimd
        def _(pool):
            nc.gpsimd.memset(nat[:, :, :], 0.0).then_inc(zeroed, 1)
            nc.gpsimd.memset(w["eps"][:, :], EPS).then_inc(zeroed, 1)
            nc.gpsimd.memset(w["xs"][:, :], 0.0).then_inc(zeroed, 1)
            pool.wait_ge(zeroed, 1)
            for i, name in ((0, "s1"), (1, "s2")):
                pool.dma_start(w["scol"][:, i:i + 1], inp[name].rearrange("(a c) -> a c", a=1).broadcast_to((128, 1))).then_inc(pool_w_in, 16)
            pool.dma_start(mask_words[:, 0, :], inp["attn_mask"].rearrange("(a w) -> a w", a=1)).then_inc(pool_w_in, 16)
            pool.dma_start(mask_words[:, 1, :], inp["ffn_mask"].rearrange("(a w) -> a w", a=1)).then_inc(pool_w_in, 16)
            for r in range(2):
                s = slice(C * r, C * r + C)
                for slot, name in ((NP, "W_p"), (NQ, "Wq"), (NK, "Wk"), (NV, "Wv")):
                    pool.dma_start(nat[s, slot, s], inp[name]).then_inc(pool_w_in, 16)
                pool.dma_start(w["bp"][s, :], inp["b_p"].rearrange("(c a) -> c a", a=1)).then_inc(pool_w_in, 16)
            n = NSTEP * NOPS
            nc.gpsimd.memset(w["code"][:, n:], 1000.0).then_inc(code_chain, 1)
            pool.wait_ge(cst_in, 16)
            pool.wait_ge(pool_w_in, 16 * 14)
            nc.gpsimd.tensor_copy(flags[:, :, :], mask_bytes[:, :, 0:NSTEP * NOPS]).then_inc(code_chain, 1)
            pool.wait_ge(code_chain, 2)
            nc.gpsimd.tensor_scalar(flags[:, 1, :], flags[:, 1, :], 2.0, None, ALU.mult).then_inc(code_chain, 1)
            pool.wait_ge(code_chain, 3)
            nc.gpsimd.tensor_tensor(flags[:, 0, :], flags[:, 0, :], flags[:, 1, :], ALU.add).then_inc(code_chain, 1)
            pool.wait_ge(code_chain, 4)
            nc.gpsimd.tensor_scalar(flags[:, 1, :], flags[:, 0, :], 0.0, 1000.0, ALU.is_equal, ALU.mult).then_inc(code_chain, 1)
            pool.wait_ge(code_chain, 5)
            nc.gpsimd.tensor_tensor(flags[:, 0, :], flags[:, 0, :], flags[:, 1, :], ALU.add).then_inc(code_chain, 1)
            pool.wait_ge(code_chain, 6)
            nc.gpsimd.tensor_tensor(w["code"][:, 0:n].rearrange("a (b o) -> a b o", o=NOPS),
                                    flags[:, 0, :].rearrange("a (b o) -> a b o", o=NOPS),
                                    cst[0:1, IOTA:IOTA + NSTEP].unsqueeze(2).broadcast_to((1, NSTEP, NOPS)), ALU.add).then_inc(code_chain, 1)

        @block.scalar
        def _(act):
            act.dma_start(cst[:, :], inp["consts"]).then_inc(cst_in, 16)
            act.wait_ge(zeroed, 1)
            for j, row in ((0, 0), (2, 64), (3, 96), (1, 32)):
                act.dma_start(nat[row:row + 32, NBC, :], inp["W_x"][DR:DR + 32, :]).then_inc(act_w_in, 16)
            act.dma_start(nat[0:DR, NX, :], inp["W_x"][0:DR, :]).then_inc(act_w_in, 16)
            act.dma_start(nat[:, NDT, 0:DR], inp["W_dt"]).then_inc(act_w_in, 16)
            act.dma_start(nat[0:C, NO, :], inp["W_out"]).then_inc(act_w_in, 16)
            act.dma_start(a_log[:, :], inp["A_log"]).then_inc(act_w_in, 16)
            act.dma_start(w["cb"][:, :], inp["conv_b"].rearrange("(d a) -> d a", a=1)).then_inc(act_w_in, 16)
            act.dma_start(w["bdt"][:, :], inp["b_dt"].rearrange("(d a) -> d a", a=1)).then_inc(act_w_in, 16)
            act.dma_start(w["dsk"][:, :], inp["D_skip"].rearrange("(d a) -> d a", a=1)).then_inc(act_w_in, 16)
            act.wait_ge(gn_chain, 4)
            act.wait_ge(zeroed, 2)
            nc.scalar.activation(gdev[:, :], gdev[:, :], ACT.Ln, bias=w["eps"][:, :]).then_inc(gsd_done, 1)
            act.wait_ge(gsd_done, 1)
            nc.scalar.activation(grs[:, :], gdev[:, :], ACT.Exp, scale=-0.5).then_inc(grs_done, 1)

            def square(b):
                act.wait_ge(dev_done, b + 1)
                atleast(act, var_done, b - 1)
                nc.scalar.activation(sq[b % 2][:, :], pd[b % 2][:, :], ACT.Square).then_inc(sq_done, 1)

            def log(b):
                act.wait_ge(var_done, b + 1)
                nc.scalar.activation(sd[b][:, :], pv[:, :], ACT.Ln, bias=w["eps"][:, :]).then_inc(sd_done, 1)

            square(0)
            for b in range(B):
                if b + 1 < B:
                    square(b + 1)
                log(b)
            act.wait_ge(act_w_in, 16 * 11)
            nc.scalar.activation(a_log[:, :], a_log[:, :], ACT.Exp).then_inc(a_exp, 1)
            act.wait_ge(sd_done, B)
            nc.scalar.activation(sd[0][:, :], sd[0][:, :], ACT.Exp, scale=-0.5).then_inc(rs_done, 1)
            act.wait_ge(w_in, 16 * 6)
            act.wait_ge(zeroed, 3)
            for b in range(B):
                if b + 1 < B:
                    nc.scalar.activation(sd[b + 1][:, :], sd[b + 1][:, :], ACT.Exp, scale=-0.5).then_inc(rs_done, 1)
                act.wait_ge(zt_done, b + 1)
                plain, shuffled = b * XW, (B + b) * XW
                nc.scalar.activation(w["xs"][C:128, plain + 4:plain + 4 + L], zt[b][0:C, :], ACT.Identity,
                                     bias=w["bet"][0:C, :], scale=w["gam"][0:C, :])
                nc.scalar.activation(w["xs"][0:C, shuffled + 3:shuffled + 3 + L], zt[b][C:128, :], ACT.Identity,
                                     bias=w["bet"][C:128, :], scale=w["gam"][C:128, :]).then_inc(act_x, 1)

        turns = [(NCA, w["wca"], 1.0), (NCB, w["wcb"], 1.0), (NG, w["wg"], 1.0), (NBC, w["wbc"], 0.5),
                 (NDT, wdtT, 1.0), (NO, w["wo"], 0.25), (NP, wpT, 1.0), (NQ, w["wq1"], 1.0),
                 (NK, w["wk1"], 1.0), (NV, w["wv1"], 1.0)]

        @block.vector
        def _(dve):
            dve.wait_ge(cst_in, 16)
            nc.vector.tensor_copy(w["sel"][:, :, :], cst[:, SELV:SELV + 32].unsqueeze(2).broadcast_to((128, 32, 128))).then_inc(sel_done, 1)
            dve.wait_ge(x_in, 16 * 9)
            for b in range(B):
                for h in range(2):
                    nc.vector.bn_stats(stats[:, b, h, :], xx[:, b * L + h * HALF:b * L + (h + 1) * HALF]).then_inc(stats_done, 1)
            dve.wait_ge(stats_done, 2 * B)
            for b in range(B):
                nc.vector.bn_aggr(mv[:, b, :], stats[:, b, :, :].rearrange("p h s -> p (h s)")).then_inc(aggr_done, 1)
            dve.wait_ge(pair_done, 1)
            nc.vector.tensor_copy(gstat[:, :, :], pg[:, 0:2 * B].rearrange("p (b s) -> p s b", s=2)).then_inc(gn_chain, 1)
            dve.wait_ge(gn_chain, 1)
            nc.vector.tensor_tensor(gdev[:, :], mv[:, :, 0], gstat[:, 0, :], ALU.subtract).then_inc(gn_chain, 1)
            dve.wait_ge(gn_chain, 2)
            nc.vector.tensor_tensor(gdev[:, :], gdev[:, :], gdev[:, :], ALU.mult).then_inc(gn_chain, 1)
            dve.wait_ge(gn_chain, 3)
            nc.vector.tensor_tensor(gdev[:, :], gdev[:, :], gstat[:, 1, :], ALU.add).then_inc(gn_chain, 1)
            dve.wait_ge(grs_done, 1)

            def group_normed(b):
                atleast(dve, dev_done, b - 1)
                nc.vector.tensor_scalar(z0[b % 2][:, :], xx[:, b * L:(b + 1) * L], gstat[:, 0, b:b + 1], grs[:, b:b + 1],
                                        ALU.subtract, ALU.mult).then_inc(z0_done, 1)

            def keep(b):
                dve.wait_ge(sq_done, b + 1)
                nc.vector.tensor_copy(zt[b][:, :], pd[b % 2][:, :]).then_inc(dev_out, 1)

            group_normed(0)
            group_normed(1)
            for b in range(B):
                keep(b)
                if b + 2 < B:
                    group_normed(b + 2)
            dve.wait_ge(w_in, 16 * 6)
            dve.wait_ge(zeroed, 1)
            for slot, lo, hi in ((NCA, 3, 2), (NCB, 1, 0)):
                for part, tap in ((0, lo), (1, hi)):
                    nc.vector.tensor_scalar(nat[:, slot, C * part:C * part + C], win[:, 0, :],
                                            conv_w[:, tap:tap + 1], None, ALU.mult).then_inc(scaled, 1)
            nc.vector.tensor_copy(nat[:, NG, 0:C], win[:, 1, :]).then_inc(scaled, 1)

            def turned_out(n):
                slot, to, by = turns[n]
                dve.wait_ge(turned, n + 1)
                nc.vector.tensor_scalar(to[:, :], pw[n % 2][:, 0:128], by, None, ALU.mult).then_inc(weight_out, 1)

            dve.wait_ge(zeroed, 3)
            for b in range(B):
                turned_out(2 * b)
                turned_out(2 * b + 1)
                if turns[2 * b][1] is wpT:
                    dve.wait_ge(weight_out, 2 * b + 1)
                    nc.vector.tensor_scalar(wpg[:, :], wpT[:, :], w["gam"][:, :], None, ALU.mult).then_inc(wpg_done, 1)
                dve.wait_ge(rs_done, b + 1)
                dve.wait_ge(dev_out, b + 1)
                nc.vector.tensor_tensor(zt[b][:, :], zt[b][:, :], sd[b][:, :], ALU.mult).then_inc(zt_done, 1)
                dve.wait_ge(zt_done, b + 1)
                plain, shuffled = b * XW, (B + b) * XW
                nc.vector.tensor_scalar(w["xs"][0:C, plain + 3:plain + 3 + L], zt[b][0:C, :], w["gam"][0:C, :],
                                        w["bet"][0:C, :], ALU.mult, ALU.add).then_inc(dve_x, 1)
                nc.vector.tensor_scalar(w["xs"][C:128, shuffled + 4:shuffled + 4 + L], zt[b][C:128, :], w["gam"][C:128, :],
                                        w["bet"][C:128, :], ALU.mult, ALU.add).then_inc(dve_x, 1)
            turned_out(8)
            turned_out(9)
            dve.wait_ge(turned, len(turns) + 1)
            nc.vector.tensor_scalar(w["wdt"][:, :], pw[0][:, 0:128], 0.5, None, ALU.mult).then_inc(weight_out, 1)
            dve.wait_ge(wp_centred, 1)
            nc.vector.tensor_copy(w["wp"][:, :], pd[0][:, 0:128])
            nc.vector.tensor_tensor(w["bp"][:, :], w["bp"][:, :], pd[0][:, 128:129], ALU.add)
            dve.wait_ge(a_exp, 1)
            nc.vector.tensor_scalar(w["aneg"][:, :], a_log[:, :], -1.0, None, ALU.mult)
            nc.vector.tensor_scalar(w["hcb"][:, :], w["cb"][:, :], 0.5, None, ALU.mult)

        @block.tensor
        def _(pe):
            pe.wait_ge(cst_in, 16)
            pe.wait_ge(aggr_done, B)
            nc.tensor.matmul(pg[:, 0:2 * B], cst[:, PAIR:PAIR + 128], mv[:, :, :].rearrange("p b s -> p (b s)"),
                             start=True, stop=True).then_inc(pair_done, 1)

            def deviations(b):
                pe.wait_ge(z0_done, b + 1)
                atleast(pe, dev_out, b - 1)
                atleast(pe, sq_done, b - 1)
                for h in range(2):
                    last = nc.tensor.matmul(pd[b % 2][:, h * HALF:(h + 1) * HALF], cst[:, CEN:CEN + 128],
                                            z0[b % 2][:, h * HALF:(h + 1) * HALF], start=True, stop=True)
                last.then_inc(dev_done, 1)

            def variances(b):
                pe.wait_ge(sq_done, b + 1)
                atleast(pe, sd_done, b)
                for h in range(2):
                    last = nc.tensor.matmul(pv[:, h * HALF:(h + 1) * HALF], cst[:, MEAN:MEAN + 128],
                                            sq[b % 2][:, h * HALF:(h + 1) * HALF], start=True, stop=True)
                last.then_inc(var_done, 1)

            deviations(0)
            for b in range(B):
                if b + 1 < B:
                    deviations(b + 1)
                variances(b)
            pe.wait_ge(scaled, 5)
            pe.wait_ge(act_w_in, 16 * 11)
            pe.wait_ge(pool_w_in, 16 * 14)
            for n, (slot, _, _) in enumerate(turns):
                atleast(pe, weight_out, n - 1)
                nc.tensor.transpose(pw[n % 2][:, 0:128], nat[:, slot, :], cst[:, IDN:IDN + 128]).then_inc(turned, 1)
            pe.wait_ge(wpg_done, 1)
            nc.tensor.matmul(pd[0][:, 0:128], cst[:, CEN:CEN + 128], wpg[:, :], start=True, stop=True)
            nc.tensor.matmul(pd[0][:, 128:129], wpT[:, :], w["bet"][:, :], start=True, stop=True).then_inc(wp_centred, 1)
            pe.wait_ge(weight_out, len(turns))
            nc.tensor.matmul(pw[0][:, 0:128], nat[:, NX, :], wdtT[:, :], start=True, stop=True).then_inc(turned, 1)


def build_scan(nc, w, inp):
    ctx = ExitStack()
    with ctx:
        def sb(name, shape, dt=FP32):
            return ctx.enter_context(nc.sbuf_tensor(name, shape, dt))

        def ps(name, shape):
            return ctx.enter_context(nc.psum_tensor(name, shape, FP32))

        def sem(name):
            return ctx.enter_context(nc.semaphore(name))

        u2 = [sb(f"u2_{i}", [DI, L]) for i in range(2)]
        gate = [sb(f"gate_{i}", [DI, L]) for i in range(2)]
        dt = [sb(f"dt_{i}", [DI, L]) for i in range(2)]
        dtu = [sb(f"dtu_{i}", [DI, L]) for i in range(2)]
        bc3 = [sb(f"bc3_{i}", [128, L], BF16) for i in range(2)]
        yg = [sb(f"yg_{i}", [DI, L]) for i in range(2)]
        da = [sb(f"da_{i}", [DI, L]) for i in range(2)]
        cc = [sb(f"cc_{i}", [DI, L]) for i in range(2)]
        hh = [sb(f"hh_{i}", [DI, L]) for i in range(2)]
        hc = [sb(f"hc_{i}", [DI, L]) for i in range(2)]
        th, xb = sb("th", [DI, L]), sb("xb", [DI, L])
        th2, xb2 = sb("th2", [DI, L]), sb("xb2", [DI, L])
        ex, one = sb("ex", [DI, L]), sb("one", [DI, L])
        ln, rl = sb("ln", [DI, L]), sb("rl", [DI, L])
        rest, yt = sb("rest", [128, L]), sb("yt", [DI, L])

        pb = [ps(f"pb_{i}", [DI, L]) for i in range(2)]
        pc = ps("pc", [DI, HALF])
        px = ps("px", [128, HALF])
        py = ps("py", [DI, L])

        b_full, c_full, c_out = sem("b_full"), sem("c_full"), sem("c_out")
        dbu_done, da_done, scan_done = sem("dbu_done"), sem("da_done"), sem("scan_done")
        hc_done, hc_used, y_free = sem("hc_done"), sem("hc_used"), sem("y_free")
        yg_done = sem("yg_done")
        px_full, px_free = sem("px_full"), sem("px_free")
        u_done, g_done, e_done, one_done, lost_done, part_done, l_done, dt_done, dtu_done = (
            sem("u_done"), sem("g_done"), sem("e_done"), sem("one_done"), sem("lost_done"), sem("part_done"),
            sem("l_done"), sem("dt_done"), sem("dtu_done"))
        bc1_done, bc_chain = sem("bc1_done"), sem("bc_chain")
        xm_done, stacked = sem("xm_done"), sem("stacked")
        res_scaled, res_added, ysum_done, act_passed = sem("res_scaled"), sem("res_added"), sem("ysum_done"), sem("act_passed")
        res2 = sb("res2", [128, HALF])
        BC_OPS = 3
        PIECES = 8
        ident, xs = w["cst"][:, IDN:IDN + 128], w["xs"]

        def half(h):
            return slice(h * HALF, (h + 1) * HALF)

        def use(q, piece, out_before):
            return PIECES * q + piece + 2 * out_before

        def kinds(q):
            return (0, 2, 3, 1) if isinstance(q, int) and q == 0 else (0, 1, 2, 3)

        def place(q, kind, h):
            return 2 * kinds(q).index(kind) + h

        def bank(q, piece):
            return pc if isinstance(q, int) and q == 0 and piece % 2 else px

        block = ctx.enter_context(nc.Block())
        pool_passed = sem("pool_passed")

        def pe_piece(pe, q, b, s, out_before, piece):
            kind, h, par = kinds(q)[piece // 2], piece % 2, s
            k = use(q, piece, out_before)
            early = isinstance(q, int) and q == 0
            px = bank(q, piece)
            atleast(pe, px_free, k - 1 if early and kinds(q)[(piece - 1) // 2] != 3 else k)
            at = (s * B + b) * XW + h * HALF
            if kind == 0:
                nc.tensor.matmul(px[:, :], w["wca"][:, :], xs[:, bass.ds(at + 3, HALF)], start=True, stop=False)
                last = nc.tensor.matmul(px[:, :], w["wcb"][:, :], xs[:, bass.ds(at + 1, HALF)], start=False, stop=True)
            elif kind == 1:
                last = nc.tensor.matmul(px[:, :], w["wg"][:, :], xs[:, bass.ds(at + 3, HALF)], start=True, stop=True)
            else:
                pe.wait_ge(u_done, 2 * q + h + 1)
                last = nc.tensor.matmul(px[:, :], (w["wdt"] if kind == 2 else w["wbc"])[:, :], u2[par][:, half(h)],
                                        start=True, stop=True)
            last.then_inc(px_full, 1)

        def pe_b(pe, u, n, par, q):
            if n == 0:
                pe.wait_ge(bc_chain, BC_OPS * (q + 1))
            atleast(pe, scan_done, u - 1)
            for h in range(2):
                last = nc.tensor.matmul(pb[n % 2][:, half(h)], w["sel"][:, n, :], bc3[par][:, half(h)], start=True, stop=True)
            last.then_inc(b_full, 1)

        def pe_c(pe, u, n, par, h):
            atleast(pe, c_out, 2 * u + h)
            if isinstance(u, int) and u == 0 and h == 0:
                pe.wait_ge(px_free, PIECES)
            nc.tensor.matmul(pc[:, :], w["sel"][:, NS + n, :], bc3[par][:, half(h)], start=True, stop=True).then_inc(c_full, 1)

        def pe_sum(pe, u, n, q, h):
            if h == 0:
                pe.wait_ge(hc_done, u + 1)
            if n == 0:
                atleast(pe, y_free, 2 * q - 1 + h)
            nc.tensor.matmul(py[:, half(h)], ident, hc[n % 2][:, half(h)], start=(n == 0), stop=(n == NS - 1)).then_inc(hc_used, 1)

        def pe_out(pe, b, h, k):
            atleast(pe, px_free, k)
            pe.wait_ge(ysum_done, b + 1)
            pe.wait_ge(res_added, 2 * b + 2)
            nc.tensor.matmul(px[:, :], w["wo"][:, :], yg[0][:, half(h)], start=True, stop=False)
            nc.tensor.matmul(px[:, :], ident, w["xm"][:, bass.ds(b * L + h * HALF, HALF)], start=False, stop=True).then_inc(px_full, 1)

        def pe_last_out(pe, b, k):
            pe.wait_ge(px_free, k)
            pe.wait_ge(c_out, 2 * NS * NSEQ)
            pe.wait_ge(res_added, 2 * b + 2)
            pe.wait_ge(yg_done, 2 * b + 2)
            for h, bank in ((0, px), (1, pc)):
                nc.tensor.matmul(bank[:, :], ident, w["xm"][:, b * L + h * HALF:b * L + (h + 1) * HALF], start=True, stop=False)
                nc.tensor.matmul(bank[:, :], w["wo"][:, :], yg[0][:, half(h)], start=False, stop=False)
            for h, bank in ((0, px), (1, pc)):
                pe.wait_ge(yg_done, 2 * b + 3 + h)
                nc.tensor.matmul(bank[:, :], w["wo"][:, :], yg[1][:, half(h)], start=False, stop=True).then_inc(px_full, 1)

        def pe_units(pe, b, s, first=False, nxt=None, out=None):
            q, par = 2 * b + s, s
            for n in range(NS):
                u = NS * q + n
                m = (n - 2) % NS
                late = not (first and n < 2)
                pe_c(pe, u, n, par, 0)
                if late:
                    pe_sum(pe, u - 2, m, q if n >= 2 else q - 1, 0)
                if n < NS - 1:
                    pe_b(pe, u + 1, n + 1, par, q)
                elif nxt:
                    pe_b(pe, u + 1, 0, nxt[1], q + 1)
                pe_c(pe, u, n, par, 1)
                if late:
                    pe_sum(pe, u - 2, m, q if n >= 2 else q - 1, 1)
                if nxt and 1 <= n <= PIECES:
                    pe_piece(pe, 2 * nxt[0] + nxt[1], *nxt, n - 1)
                if out and n in (10, 11):
                    pe_out(pe, out[0], n - 10, out[1] + n - 10)

        @block.tensor
        def _(pe):
            for piece in range(PIECES):
                pe_piece(pe, 0, 0, 0, 0, piece)
            pe_b(pe, 0, 0, 0, 0)
            pe_units(pe, 0, 0, first=True, nxt=(0, 1, 0))
            with pe.Fori(0, B - 1) as b:
                pe_units(pe, b, 1, nxt=(b + 1, 0, b))
                pe_units(pe, b + 1, 0, nxt=(b + 1, 1, b), out=(b, use(2 * b + 4, 0, b)))
            b = B - 1
            pe_units(pe, b, 1)
            u = NS * NSEQ
            for back in (2, 1):
                for h in range(2):
                    pe_sum(pe, u - back, NS - back, NSEQ - 1, h)
            pe_last_out(pe, b, use(NSEQ, 0, b))

        def act_piece(act, q, par, out_before, piece):
            kind, h = kinds(q)[piece // 2], piece % 2
            px = bank(q, piece)
            k = use(q, piece, out_before)
            act.wait_ge(px_full, k + 1)
            if kind == 0:
                atleast(act, u_done, 2 * q + h - 1)
                nc.scalar.activation(th[:, half(h)], px[:, :], ACT.Tanh, bias=w["hcb"][:, :], scale=0.5)
                nc.scalar.activation(xb[:, half(h)], px[:, :], ACT.Identity, bias=w["cb"][:, :]).then_inc(px_free, 1)
            elif kind == 1:
                atleast(act, g_done, 2 * q + h - 1)
                nc.scalar.activation(th2[:, half(h)], px[:, :], ACT.Tanh, scale=0.5)
                nc.scalar.activation(xb2[:, half(h)], px[:, :], ACT.Identity).then_inc(px_free, 1)
            elif kind == 2:
                atleast(act, dt_done, q)
                nc.scalar.activation(ex[:, half(h)], px[:, :], ACT.Abs, bias=w["bdt"][:, :])
                nc.scalar.activation(rl[:, half(h)], px[:, :], ACT.Relu, bias=w["bdt"][:, :]).then_inc(px_free, 1)
            else:
                nc.scalar.activation(bc3[par][:, half(h)], px[:, :], ACT.Copy).then_inc(bc1_done, 1)

        def act_one(act, q, out_before, h):
            act.wait_ge(px_free, use(q, place(q, 2, h), out_before) + 1)
            nc.scalar.activation(ex[:, half(h)], ex[:, half(h)], ACT.Exp, scale=-1.0).then_inc(e_done, 1)
            act.wait_ge(e_done, 2 * q + h + 1)
            nc.scalar.activation(one[:, half(h)], ex[:, half(h)], ACT.Identity, bias=1.0).then_inc(one_done, 1)

        def act_ln(act, q):
            act.wait_ge(one_done, 2 * q + 2)
            nc.scalar.activation(ln[:, :], one[:, :], ACT.Ln).then_inc(l_done, 1)

        def act_exp(act, u, n, par, q):
            if n == 0:
                act.wait_ge(dt_done, q + 1)
            atleast(act, scan_done, u - 1)
            nc.scalar.activation(da[n % 2][:, :], dt[par][:, :], ACT.Exp, scale=w["aneg"][:, n:n + 1]).then_inc(da_done, 1)

        def act_c(act, u, n, h):
            act.wait_ge(c_full, 2 * u + h + 1)
            if h == 0:
                atleast(act, hc_done, u - 1)
            nc.scalar.activation(cc[n % 2][:, half(h)], pc[:, :], ACT.Copy).then_inc(c_out, 1)

        def act_out(act, b, h, k, bank=px):
            if isinstance(k, int):
                act.wait_ge(px_full, k + 1)
            else:
                settle(act, px_full, k + 1, act_passed)
            nc.scalar.activation(w["xm"][0:C, bass.ds(b * L + h * HALF, HALF)], bank[0:C, :], ACT.Copy).then_inc(px_free, 1)

        def act_residual(act, b, h):
            if h:
                settle(act, res_added, 2 * b + h, act_passed)
            for i, to in ((0, w["xm"][:, bass.ds(b * L + h * HALF, HALF)]), (1, res2[:, :])):
                last = nc.scalar.activation(to, xs[:, bass.ds((i * B + b) * XW + 3 + h * HALF, HALF)], ACT.Copy,
                                            scale=w["scol"][:, i:i + 1])
            last.then_inc(res_scaled, 1)

        def act_units(act, b, s, nxt=None, out=None):
            q, par = 2 * b + s, s
            for n in range(NS):
                u = NS * q + n
                act_c(act, u, n, 0)
                if nxt and 2 <= n <= PIECES + 1:
                    act_piece(act, 2 * nxt[0] + nxt[1], nxt[1], nxt[2], n - 2)
                if out and n in (11, 12):
                    act_out(act, out[0], n - 11, out[1] + n - 11)
                if s == 1 and n in (12, 14):
                    act_residual(act, b, (n - 12) // 2)
                act_c(act, u, n, 1)
                if n < NS - 1:
                    act_exp(act, u + 1, n + 1, par, q)
                elif nxt:
                    act_exp(act, u + 1, 0, nxt[1], q + 1)
                if nxt and n in (6, 7):
                    act_one(act, 2 * nxt[0] + nxt[1], nxt[2], n - 6)
                if nxt and n == 10:
                    act_ln(act, 2 * nxt[0] + nxt[1])

        @block.scalar
        def _(act):
            for piece in range(PIECES):
                if piece == 6:
                    act_ln(act, 0)
                act_piece(act, 0, 0, 0, piece)
                if piece in (2, 3):
                    act_one(act, 0, 0, piece - 2)
            act_exp(act, 0, 0, 0, 0)
            act_units(act, 0, 0, nxt=(0, 1, 0))
            with act.Fori(0, B - 1) as b:
                act_units(act, b, 1, nxt=(b + 1, 0, b))
                act_units(act, b + 1, 0, nxt=(b + 1, 1, b), out=(b, use(2 * b + 4, 0, b)))
            b = B - 1
            act_units(act, b, 1)
            for h in range(2):
                act_out(act, b, h, use(NSEQ, 0, b) + h, (px, pc)[h])
            act.drain().then_inc(xm_done, 1)

        def dve_piece(dve, q, par, out_before, piece):
            kind, h = kinds(q)[piece // 2], piece % 2
            px = bank(q, piece)
            k = use(q, piece, out_before)
            if kind == 0:
                dve.wait_ge(px_free, k + 1)
                atleast(dve, yg_done, q)
                nc.vector.scalar_tensor_tensor(u2[par][:, half(h)], th[:, half(h)], 1.0, xb[:, half(h)],
                                               ALU.add, ALU.mult).then_inc(u_done, 1)
            elif kind == 1:
                dve.wait_ge(px_free, k + 1)
                atleast(dve, yg_done, q)
                nc.vector.scalar_tensor_tensor(gate[par][:, half(h)], th2[:, half(h)], 1.0, xb2[:, half(h)],
                                               ALU.add, ALU.mult).then_inc(g_done, 1)
            elif kind == 3:
                dve.wait_ge(bc1_done, 2 * q + h + 1)
                if h == 0:
                    atleast(dve, bc_chain, BC_OPS * q)
                nc.vector.tensor_tensor(rest[64:128, half(h)], px[64:128, :], bc3[par][64:128, half(h)],
                                        ALU.subtract).then_inc(px_free, 1)

        def dve_lost(dve, q):
            dve.wait_ge(one_done, 2 * q + 2)
            nc.vector.scalar_tensor_tensor(ex[:, :], one[:, :], 1.0, ex[:, :], ALU.subtract, ALU.subtract).then_inc(lost_done, 1)

        def dve_parts(dve, q, par, out_before):
            dve.wait_ge(px_free, use(q, place(q, 3, 1), out_before) + 1)
            base = BC_OPS * q
            nc.vector.tensor_copy(bc3[par][64:128, :], rest[64:128, :]).then_inc(bc_chain, 1)
            dve.wait_ge(bc_chain, base + 1)
            nc.vector.tensor_tensor(rest[96:128, :], rest[96:128, :], bc3[par][96:128, :], ALU.subtract).then_inc(bc_chain, 1)
            dve.wait_ge(bc_chain, base + 2)
            nc.vector.tensor_copy(bc3[par][96:128, :], rest[96:128, :]).then_inc(bc_chain, 1)

        def dve_dt(dve, q, par):
            dve.wait_ge(l_done, q + 1)
            dve.wait_ge(part_done, q + 1)
            atleast(dve, da_done, NS * (q - 1))
            nc.vector.tensor_tensor(dt[par][:, :], ln[:, :], rl[:, :], ALU.add).then_inc(dt_done, 1)

        def dve_dtu(dve, q, par):
            dve.wait_ge(dt_done, q + 1)
            atleast(dve, dbu_done, NS * (q - 1))
            nc.vector.tensor_tensor(dtu[par][:, :], dt[par][:, :], u2[par][:, :], ALU.mult).then_inc(dtu_done, 1)

        def dve_unit(dve, u, n, par, q):
            dve.wait_ge(b_full, u + 1)
            if n == 0:
                dve.wait_ge(dtu_done, q + 1)
            nc.vector.tensor_tensor(pb[n % 2][:, :], pb[n % 2][:, :], dtu[par][:, :], ALU.mult).then_inc(dbu_done, 1)
            dve.wait_ge(da_done, u + 1)
            dve.wait_ge(dbu_done, u + 1)
            atleast(dve, hc_done, u - 1)
            nc.vector.tensor_tensor_scan(hh[n % 2][:, :], da[n % 2][:, :], pb[n % 2][:, :], 0.0,
                                         ALU.mult, ALU.add).then_inc(scan_done, 1)

        def dve_y(dve, q, s, h):
            dve.wait_ge(hc_used, 2 * NS * (q + 1) - 1 + h)
            if h == 0:
                dve.wait_ge(yg_done, q + 1)
            nc.vector.scalar_tensor_tensor(yt[:, half(h)], u2[s][:, half(h)], w["dsk"][:, :], py[:, half(h)],
                                           ALU.mult, ALU.add).then_inc(y_free, 1)

        def dve_units(dve, b, s, nxt=None, prev=None):
            q, par = 2 * b + s, s
            for n in range(NS):
                u = NS * q + n
                if prev and n == 2:
                    for h in range(2):
                        dve_y(dve, q - 1, prev[1], h)
                dve_unit(dve, u, n, par, q)
                if nxt:
                    qn = 2 * nxt[0] + nxt[1]
                    if 3 <= n <= 6:
                        dve_piece(dve, qn, nxt[1], nxt[2], n - 3)
                    if n in (8, 9):
                        dve_piece(dve, qn, nxt[1], nxt[2], n - 2)
                    if n == 8:
                        dve_lost(dve, qn)
                    if n == 10:
                        dve_parts(dve, qn, nxt[1], nxt[2])
                    if n == 12:
                        dve_dt(dve, qn, nxt[1])
                    if n == 13:
                        dve_dtu(dve, qn, nxt[1])

        @block.vector
        def _(dve):
            for piece in range(PIECES - 2):
                dve_piece(dve, 0, 0, 0, piece)
                if piece == 3:
                    dve_lost(dve, 0)
            dve_parts(dve, 0, 0, 0)
            dve_dt(dve, 0, 0)
            dve_dtu(dve, 0, 0)
            for piece in (PIECES - 2, PIECES - 1):
                dve_piece(dve, 0, 0, 0, piece)
            dve_units(dve, 0, 0, nxt=(0, 1, 0))
            with dve.Fori(0, B - 1) as b:
                dve_units(dve, b, 1, nxt=(b + 1, 0, b), prev=(b, 0))
                dve_units(dve, b + 1, 0, nxt=(b + 1, 1, b), prev=(b, 1))
            b = B - 1
            dve_units(dve, b, 1, prev=(b, 0))
            for h in range(2):
                dve_y(dve, NSEQ - 1, 1, h)
                dve.wait_ge(y_free, 2 * NSEQ - 1 + h)
                nc.vector.tensor_tensor(yg[1][:, half(h)], yt[:, half(h)], gate[1][:, half(h)], ALU.mult).then_inc(yg_done, 1)

        def pool_hc(pool, u, n):
            pool.wait_ge(scan_done, u + 1)
            pool.wait_ge(c_out, 2 * u + 2)
            atleast(pool, hc_used, 2 * (u - 1))
            nc.gpsimd.tensor_tensor(hc[n % 2][:, :], hh[n % 2][:, :], cc[n % 2][:, :], ALU.mult).then_inc(hc_done, 1)

        def pool_dt(pool, q):
            settle(pool, lost_done, q + 1, pool_passed)
            nc.gpsimd.tensor_tensor(rl[:, :], rl[:, :], ex[:, :], ALU.subtract).then_inc(part_done, 1)

        def pool_gate(pool, q, s, b):
            pool.wait_ge(y_free, 2 * q + 2)
            atleast(pool, px_free, use(2 * b + 2, 0, b - 1) + 2 if not isinstance(b, int) or b > 0 else 0)
            nc.gpsimd.tensor_tensor(yg[s][:, :], yt[:, :], gate[s][:, :], ALU.mult).then_inc(yg_done, 1)

        def pool_ysum(pool, q):
            pool.wait_ge(yg_done, q + 2)
            nc.gpsimd.tensor_tensor(yg[0][:, :], yg[0][:, :], yg[1][:, :], ALU.add).then_inc(ysum_done, 1)

        def pool_residual(pool, b, h):
            settle(pool, res_scaled, 2 * b + h + 1, pool_passed)
            at = w["xm"][:, bass.ds(b * L + h * HALF, HALF)]
            nc.gpsimd.tensor_tensor(at, at, res2[:, :], ALU.add).then_inc(res_added, 1)

        def pool_units(pool, b, s, nxt=None, prev=None):
            q = 2 * b + s
            for n in range(NS):
                pool_hc(pool, NS * q + n, n)
                if prev and n == 2:
                    pool_gate(pool, q - 1, prev[1], prev[0])
                if prev and n == 5 and prev[1] == 1:
                    pool_ysum(pool, q - 1)
                if nxt and n == 8:
                    pool_dt(pool, 2 * nxt[0] + nxt[1])
                if s == 1 and n in (12, 14):
                    pool_residual(pool, b, (n - 12) // 2)

        @block.gpsimd
        def _(pool):
            pool.sem_inc(yg_done, 1)
            pool_dt(pool, 0)
            pool_units(pool, 0, 0, nxt=(0, 1, 0))
            with pool.Fori(0, B - 1) as b:
                pool_units(pool, b, 1, nxt=(b + 1, 0, b), prev=(b, 0))
                pool_units(pool, b + 1, 0, nxt=(b + 1, 1, b), prev=(b, 1))
            pool_units(pool, B - 1, 1, prev=(B - 1, 0))

        @block.sync
        def _(sp):
            xm = w["xm"][0:C, :].rearrange("c (p r t) -> c r p t", p=2, r=2)
            xm2 = w["xm2"][:, :].rearrange("c (p t) -> c p t", p=2)
            sp.wait_ge(px_free, use(2 * B, 0, B - 2) + 2)
            sp.dma_start(xm2[0:C, :, :], xm[:, 0, :, :]).then_inc(stacked, 16)
            sp.dma_start(xm2[C:128, 0, :], xm[:, 1, 0, :]).then_inc(stacked, 16)
            sp.wait_ge(xm_done, 1)
            sp.dma_start(xm2[C:128, 1, :], xm[:, 1, 1, :]).then_inc(stacked, 16)
            sp.wait_ge(stacked, 48)


class Attention:

    GRP = T2C // 128

    def __init__(self, nc, ctx, w, causal):
        tag = "l1_" if causal else "ex_"

        def sb(name, shape):
            return ctx.enter_context(nc.sbuf_tensor(tag + name, shape, FP32))

        def ps(name, shape):
            return ctx.enter_context(nc.psum_tensor(tag + name, shape, FP32))

        self.nc, self.w, self.causal = nc, w, causal
        self.qt, self.kt = sb("qt", [128, T2C]), sb("kt", [128, T2C])
        self.vv = sb("vv", [128, self.GRP, 2, VW])
        self.qs = [sb(f"qs_{r}", [128, 128]) for r in range(2)]
        self.p = [sb(f"p_{r}", [128, L]) for r in range(2)]
        self.pts = [sb(f"pts_{r}", [128, L]) for r in range(2)]
        self.o2 = sb("o2", [128, 2, C])
        self.mx, self.nm, self.rc = sb("mx", [128, 2]), sb("nm", [128, 2]), sb("rc", [128, 2])
        self.s = [ps(f"s_{r}", [128, L]) for r in range(2)]
        self.pt = [ps(f"pt_{j}", [128, HALF]) for j in range(2)]
        self.ob = [ps(f"ob_{r}", [128, HALF]) for r in range(2)]
        names = ("at_zero", "qk_full", "q_out", "k_out", "v_full", "v_out0", "v_out1", "qs_ready", "s_full", "mx_done",
                 "nm_done", "p_done", "tr0", "tr1", "pt0_out", "pt1_out", "o_full", "rc_done", "o_out", "ot_full", "ot_out")
        self.passed = ctx.enter_context(nc.semaphore(tag + "passed"))
        (self.at_zero, self.qk_full, self.q_out, self.k_out, self.v_full, self.v_out0, self.v_out1, self.qs_ready,
         self.s_full, self.mx_done, self.nm_done, self.p_done, self.tr0, self.tr1, self.pt0_out, self.pt1_out,
         self.o_full, self.rc_done, self.o_out, self.ot_full, self.ot_out) = (
            ctx.enter_context(nc.semaphore(tag + name)) for name in names)

    def prime(self, eng, *counts):
        for sem, count in counts:
            eng.sem_inc(sem, count)

    def prime_pe(self, pe):
        tiles = 2 * self.GRP
        self.prime(pe, (self.qk_full, 8), (self.v_full, 4), (self.s_full, tiles), (self.tr0, tiles), (self.tr1, tiles),
                   (self.o_full, tiles), (self.ot_full, self.GRP))

    def prime_act(self, act):
        tiles = 2 * self.GRP
        self.prime(act, (self.q_out, 4), (self.v_out1, 2), (self.p_done, tiles), (self.pt1_out, tiles))

    def prime_dve(self, dve):
        tiles = 2 * self.GRP
        self.prime(dve, (self.k_out, 4), (self.v_out0, 2), (self.mx_done, tiles), (self.nm_done, tiles),
                   (self.pt0_out, tiles), (self.rc_done, tiles), (self.o_out, tiles), (self.ot_out, self.GRP))

    def prime_pool(self, pool):
        self.prime(pool, (self.qs_ready, 2 * self.GRP))

    def before(self, eng, sem, k, g, value):
        if not (isinstance(g, int) and g == 0 and (self.causal is False or value <= 0)):
            atleast(eng, sem, value)

    def blocks(self, i):
        return i + 1 if self.causal else L // 128

    def seconds(self, k, g, i, r):
        if not self.causal:
            return 2 * self.GRP * k + 2 * g + r
        return (g - i) + 2 * (i - 4) + r

    def prepare_pool(self, pool):
        nc = self.nc
        nc.gpsimd.memset(self.vv[:, :, :, :], 1.0).then_inc(self.at_zero, 1)
        for r in range(2):
            nc.gpsimd.memset(self.qs[r][:, :], 0.0).then_inc(self.at_zero, 1)

    def pe_project(self, pe, k, src, src_wait, wq, wk, wv):
        nc = self.nc
        for c in range(4):
            src_wait(pe, c)
            for m, (wt, out) in enumerate(((wq, self.q_out), (wk, self.k_out))):
                atleast(pe, out, 4 * k + c)
                nc.tensor.matmul(self.pt[m][:, :], wt[:, :], src[:, c * HALF:(c + 1) * HALF],
                                 start=True, stop=True).then_inc(self.qk_full, 1)
        for m in range(self.GRP // 4):
            atleast(pe, (self.v_out0, self.v_out1)[m % 2], 2 * k + m // 2)
            for j in range(4):
                g = 4 * m + j
                last = nc.tensor.matmul(self.ob[m % 2][:, j * 128:(j + 1) * 128], src[:, g * 128:(g + 1) * 128],
                                        wv[:, :], start=True, stop=True)
            last.then_inc(self.v_full, 1)

    def act_project(self, act, k):
        nc = self.nc
        for c in range(4):
            act.wait_ge(self.qk_full, 8 * k + 2 * c + 1)
            nc.scalar.activation(self.qt[:, c * HALF:(c + 1) * HALF], self.pt[0][:, :], ACT.Copy).then_inc(self.q_out, 1)
        act.wait_ge(self.at_zero, 3)
        for m in (1, 3):
            act.wait_ge(self.v_full, 4 * k + m + 1)
            nc.scalar.activation(self.values(m), self.ob[1][:, :].rearrange("p (g c) -> p g c", c=C),
                                 ACT.Copy).then_inc(self.v_out1, 1)

    def values(self, m):
        return self.vv[:, 4 * m:4 * m + 4, :, :].rearrange("p g r c -> p (g r) c")[:, :, 0:C]

    def dve_project(self, dve, k):
        nc = self.nc
        for c in range(4):
            dve.wait_ge(self.qk_full, 8 * k + 2 * c + 2)
            nc.vector.tensor_copy(self.kt[:, c * HALF:(c + 1) * HALF], self.pt[1][:, :]).then_inc(self.k_out, 1)
        dve.wait_ge(self.at_zero, 3)
        for m in (0, 2):
            dve.wait_ge(self.v_full, 4 * k + m + 1)
            nc.vector.tensor_copy(self.values(m), self.ob[0][:, :].rearrange("p (g c) -> p g c", c=C)).then_inc(self.v_out0, 1)

    def pe_scores(self, pe, k, g, i, p, r):
        nc, t = self.nc, 2 * (self.GRP * k + g) + r
        pe.wait_ge(self.qs_ready, t + 1)
        self.before(pe, self.p_done, k, g, t - 1)
        full = i * 128 if self.causal else L
        parts = [(a, min(HALF, full - a)) for a in range(0, full, HALF)]
        for a, n in parts:
            last = nc.tensor.matmul(self.s[r][:, a:a + n], self.qs[r][:, :], self.kt[:, bass.ds(p * L + a, n)],
                                    start=True, stop=True)
        if self.causal:
            nc.tensor.matmul(self.s[r][:, full:full + 128], self.qs[r][:, :], self.kt[:, bass.ds(p * L + full, 128)],
                             start=True, stop=False)
            last = nc.tensor.matmul(self.s[r][:, full:full + 128], self.w["cst"][:, IDN:IDN + 128],
                                    self.w["cst"][:, CAUS:CAUS + 128], start=False, stop=True)
        last.then_inc(self.s_full, 1)

    def pe_turn(self, pe, k, g, i, r):
        nc, t, n = self.nc, 2 * (self.GRP * k + g) + r, self.blocks(i)
        pe.wait_ge(self.p_done, t + 1)
        if isinstance(k, int) and isinstance(g, int) and k == 0 and g == 0 and r == 0:
            pe.wait_ge(self.k_out, 4)
        for j in range(min(n, 4)):
            if j == 0:
                atleast(pe, self.pt0_out, t)
            last = nc.tensor.transpose(self.pt[0][:, j * 128:(j + 1) * 128], self.p[r][:, j * 128:(j + 1) * 128],
                                       self.w["cst"][:, IDN:IDN + 128])
        last.then_inc(self.tr0, 1)
        for j in range(4, n):
            if j == 4:
                atleast(pe, self.pt1_out, self.seconds(k, g, i, r))
            last = nc.tensor.transpose(self.pt[1][:, (j - 4) * 128:(j - 3) * 128], self.p[r][:, j * 128:(j + 1) * 128],
                                       self.w["cst"][:, IDN:IDN + 128])
        if n > 4:
            last.then_inc(self.tr1, 1)

    def pe_values(self, pe, k, g, i, p, r):
        nc, t, n = self.nc, 2 * (self.GRP * k + g) + r, self.blocks(i)
        pe.wait_ge(self.pt0_out, t + 1)
        if n > 4:
            pe.wait_ge(self.pt1_out, self.seconds(k, g, i, r) + 1)
        self.before(pe, self.o_out, k, g, t - 1)
        for j in range(n):
            last = nc.tensor.matmul(self.ob[r][:, 0:VW], self.pts[r][:, j * 128:(j + 1) * 128],
                                    self.vv[:, bass.ds(p * 8 + j, 1), r, :].rearrange("p a c -> p (a c)"),
                                    start=(j == 0), stop=(j == n - 1))
        last.then_inc(self.o_full, 1)

    def pe_back(self, pe, k, g):
        nc, n = self.nc, self.GRP * k + g
        pe.wait_ge(self.o_out, 2 * n + 2)
        atleast(pe, self.ot_out, n)
        nc.tensor.transpose(self.ob[1][:, 256:384], self.o2[:, :, :].rearrange("p r c -> p (r c)"),
                            self.w["cst"][:, IDN:IDN + 128]).then_inc(self.ot_full, 1)

    def pe_group(self, pe, k, g, i, p, prev):
        for r in range(2):
            self.pe_scores(pe, k, g, i, p, r)
            if prev:
                self.pe_values(pe, k, prev[0], prev[1], prev[2], r)
            if r == 0 and prev:
                self.pe_turn(pe, k, prev[0], prev[1], 1)
            if r == 1:
                self.pe_turn(pe, k, g, i, 0)
        if prev:
            self.pe_back(pe, k, prev[0])

    def pe_tail(self, pe, k, g, i, p):
        self.pe_values(pe, k, g, i, p, 0)
        self.pe_turn(pe, k, g, i, 1)
        self.pe_values(pe, k, g, i, p, 1)
        self.pe_back(pe, k, g)

    def dve_max(self, dve, k, g, i, r):
        nc, t = self.nc, 2 * (self.GRP * k + g) + r
        dve.wait_ge(self.s_full, t + 1)
        self.before(dve, self.nm_done, k, g, t - 1)
        nc.vector.reduce_max(self.mx[:, r:r + 1], self.s[r][:, 0:128 * self.blocks(i)], AX.X).then_inc(self.mx_done, 1)
        dve.wait_ge(self.mx_done, t + 1)
        self.before(dve, self.p_done, k, g, t - 1)
        nc.vector.tensor_scalar(self.nm[:, r:r + 1], self.mx[:, r:r + 1], -SCALE, None, ALU.mult).then_inc(self.nm_done, 1)

    def dve_turned(self, dve, k, g, i, r):
        nc, t = self.nc, 2 * (self.GRP * k + g) + r
        n = 128 * min(self.blocks(i), 4)
        dve.wait_ge(self.tr0, t + 1)
        self.before(dve, self.o_full, k, g, t - 1)
        nc.vector.tensor_copy(self.pts[r][:, 0:n], self.pt[0][:, 0:n]).then_inc(self.pt0_out, 1)

    def dve_output(self, dve, k, g, r):
        nc, t = self.nc, 2 * (self.GRP * k + g) + r
        dve.wait_ge(self.o_full, t + 1)
        self.before(dve, self.o_out, k, g, t - 1)
        nc.vector.reciprocal(self.rc[:, r:r + 1], self.ob[r][:, C:C + 1]).then_inc(self.rc_done, 1)
        dve.wait_ge(self.rc_done, t + 1)
        if r == 0:
            atleast(dve, self.ot_full, self.GRP * k + g)
        nc.vector.tensor_scalar(self.o2[:, r, :], self.ob[r][:, 0:C], self.rc[:, r:r + 1], None, ALU.mult).then_inc(self.o_out, 1)

    def dve_group(self, dve, k, g, i, prev, finish):
        for r in range(2):
            self.dve_max(dve, k, g, i, r)
            if prev:
                self.dve_output(dve, k, prev[0], r)
            if r == 0 and prev:
                self.dve_turned(dve, k, prev[0], prev[1], 1)
            if r == 1:
                self.dve_turned(dve, k, g, i, 0)
        if prev:
            finish(dve, k, prev[0])

    def dve_tail(self, dve, k, g, i, finish):
        self.dve_output(dve, k, g, 0)
        self.dve_turned(dve, k, g, i, 1)
        self.dve_output(dve, k, g, 1)
        finish(dve, k, g)

    def act_exp(self, act, k, g, i, r):
        nc, t, n = self.nc, 2 * (self.GRP * k + g) + r, 128 * self.blocks(i)
        act.wait_ge(self.nm_done, t + 1)
        self.before(act, self.tr0, k, g, t - 1)
        if not self.causal:
            self.before(act, self.tr1, k, g, t - 1)
        elif i > 4:
            act.wait_ge(self.tr1, self.seconds(k, g, i, r) - 1)
        nc.scalar.activation(self.p[r][:, 0:n], self.s[r][:, 0:n], ACT.Exp, bias=self.nm[:, r:r + 1],
                             scale=SCALE).then_inc(self.p_done, 1)

    def act_turned(self, act, k, g, i, r):
        nc, t = self.nc, 2 * (self.GRP * k + g) + r
        n = 128 * (self.blocks(i) - 4)
        if n <= 0:
            return
        act.wait_ge(self.tr1, self.seconds(k, g, i, r) + 1)
        self.before(act, self.o_full, k, g, t - 1)
        nc.scalar.activation(self.pts[r][:, HALF:HALF + n], self.pt[1][:, 0:n], ACT.Copy).then_inc(self.pt1_out, 1)

    def act_group(self, act, k, g, i, prev):
        self.act_exp(act, k, g, i, 0)
        if prev:
            self.act_turned(act, k, prev[0], prev[1], 1)
        self.act_exp(act, k, g, i, 1)
        self.act_turned(act, k, g, i, 0)

    def pool_group(self, pool, k, g):
        nc = self.nc
        for r in range(2):
            t = 2 * (self.GRP * k + g) + r
            self.before(pool, self.s_full, k, g, t - 1)
            if not (isinstance(t, int) and t == 0):
                settle(pool, self.qs_ready, t, self.passed)
            rows = slice(C * r, C * r + C)
            nc.gpsimd.tensor_copy(self.qs[r][rows, :], self.qt[rows, bass.ds(g * 128, 128)]).then_inc(self.qs_ready, 1)

    def each(self, eng, group, tail):
        half = self.GRP // 2
        if self.causal:
            prev = None
            for p in range(2):
                for i in range(half):
                    group(p * half + i, i, p, prev)
                    prev = (p * half + i, i, p)
            tail(*prev)
            return
        group(0, 0, 0, None)
        group(1, 0, 0, (0, 0, 0))
        with eng.Fori(2, half) as g:
            group(g, 0, 0, (g - 1, 0, 0))
        group(half, 0, 1, (half - 1, 0, 0))
        with eng.Fori(half + 1, 2 * half) as g:
            group(g, 0, 1, (g - 1, 0, 1))
        tail(self.GRP - 1, 0, 1)

    def pe_all(self, pe, k):
        if isinstance(k, int):
            pe.wait_ge(self.at_zero, 3)
        pe.wait_ge(self.k_out, 4 * k + 4)
        pe.wait_ge(self.v_out0, 2 * k + 2)
        pe.wait_ge(self.v_out1, 2 * k + 2)
        self.each(pe, lambda g, i, p, prev: self.pe_group(pe, k, g, i, p, prev), lambda g, i, p: self.pe_tail(pe, k, g, i, p))

    def act_all(self, act, k):
        self.each(act, lambda g, i, p, prev: self.act_group(act, k, g, i, prev), lambda g, i, p: self.act_turned(act, k, g, i, 1))

    def dve_all(self, dve, k, finish):
        self.each(dve, lambda g, i, p, prev: self.dve_group(dve, k, g, i, prev, finish),
                  lambda g, i, p: self.dve_tail(dve, k, g, i, finish))

    def pool_all(self, pool, k):
        pool.wait_ge(self.q_out, 4 * k + 4)
        self.pool_group(pool, k, 0)
        with pool.Fori(1, self.GRP) as g:
            self.pool_group(pool, k, g)


def build_attend(nc, w, inp):
    ctx = ExitStack()
    with ctx:
        def sb(name, shape):
            return ctx.enter_context(nc.sbuf_tensor(name, shape, FP32))

        def sem(name):
            return ctx.enter_context(nc.semaphore(name))

        at = Attention(nc, ctx, w, causal=True)
        za, t1, zq = sb("za", [128, T2C]), sb("t1", [128, T2C]), sb("zq", [128, T2C])
        sq, sd = sb("lsq", [128, T2C]), sb("lsd", [128, T2C])
        ln_dev, ln_sq, ln_var, ln_sd, ln_rs, ln_z = (sem("ln_dev"), sem("ln_sq"), sem("ln_var"), sem("ln_sd"), sem("ln_rs"), sem("ln_z"))
        wp_full, t1_done = sem("wp_full"), sem("t1_done")
        NCH = T2C // HALF

        def col(c):
            return slice(c * HALF, (c + 1) * HALF)

        dev_at = [at.s[0][:, 0:HALF], at.s[0][:, HALF:L], at.ob[0][:, :], at.ob[1][:, :]]
        var_at = [at.s[1][:, 0:HALF], at.s[1][:, HALF:L], at.pt[0][:, :], at.pt[1][:, :]]

        def pe_norm(pe, call, src, ready, after=None):
            for c in range(NCH):
                ready(pe, c)
                nc.tensor.matmul(dev_at[c], w["cst"][:, CEN:CEN + 128], src[:, col(c)],
                                 start=True, stop=True).then_inc(ln_dev, 1)
            for c in range(NCH):
                pe.wait_ge(ln_sq, NCH * call + c + 1)
                nc.tensor.matmul(var_at[c], w["cst"][:, MEAN:MEAN + 128], sq[:, col(c)],
                                 start=True, stop=True).then_inc(ln_var, 1)
            if after:
                after()

        def act_norm(act, call):
            for c in range(NCH):
                act.wait_ge(ln_dev, NCH * call + c + 1)
                nc.scalar.activation(sq[:, col(c)], dev_at[c], ACT.Square).then_inc(ln_sq, 1)
            for c in range(NCH):
                act.wait_ge(ln_var, NCH * call + c + 1)
                nc.scalar.activation(sd[:, col(c)], var_at[c], ACT.Ln, bias=w["eps"][:, :]).then_inc(ln_sd, 1)
            for c in range(NCH):
                act.wait_ge(ln_sd, NCH * call + c + 1)
                nc.scalar.activation(sd[:, col(c)], sd[:, col(c)], ACT.Exp, scale=-0.5).then_inc(ln_rs, 1)

        def dve_norm(dve, call, dst):
            for c in range(NCH):
                n = NCH * call + c
                dve.wait_ge(ln_rs, n + 1)
                nc.vector.tensor_tensor(dst[:, col(c)], dev_at[c], sd[:, col(c)], ALU.mult).then_inc(ln_z, 1)

        block = ctx.enter_context(nc.Block())

        @block.gpsimd
        def _(pool):
            at.prepare_pool(pool)
            pool.wait_ge(at.at_zero, 3)
            at.pool_all(pool, 0)

        @block.tensor
        def _(pe):
            def project():
                for c in range(NCH):
                    nc.tensor.matmul(dev_at[c], w["wp"][:, :], w["xm2"][:, col(c)], start=True, stop=True).then_inc(wp_full, 1)

            pe_norm(pe, 0, w["xm2"], lambda eng, c: None, project)
            pe_norm(pe, 1, t1, lambda eng, c: eng.wait_ge(t1_done, c + 1))
            at.pe_project(pe, 0, zq, lambda eng, c: eng.wait_ge(ln_z, NCH + c + 1), w["wq1"], w["wk1"], w["wv1"])
            at.pe_all(pe, 0)
            pe_norm(pe, 2, w["t2"], lambda eng, c: eng.wait_ge(at.ot_out, at.GRP))

        @block.scalar
        def _(act):
            act_norm(act, 0)
            act_norm(act, 1)
            at.act_project(act, 0)
            at.act_all(act, 0)
            act_norm(act, 2)

        @block.vector
        def _(dve):
            for c in range(NCH):
                dve.wait_ge(ln_rs, c + 1)
                dve.wait_ge(wp_full, c + 1)
                nc.vector.tensor_tensor(za[:, col(c)], dev_at[c], sd[:, col(c)], ALU.mult).then_inc(ln_z, 1)
                dve.wait_ge(ln_z, c + 1)
                nc.vector.scalar_tensor_tensor(t1[:, col(c)], za[:, col(c)], w["bp"][:, :], w["xst"][:, col(c)],
                                               ALU.add, ALU.add).then_inc(t1_done, 1)
            dve_norm(dve, 1, zq)
            at.dve_project(dve, 0)

            def finish(eng, k, g):
                eng.wait_ge(at.ot_full, g + 1)
                nc.vector.tensor_tensor(w["t2"][:, bass.ds(g * 128, 128)], at.ob[1][:, 256:384], t1[:, bass.ds(g * 128, 128)],
                                        ALU.add).then_inc(at.ot_out, 1)

            at.dve_all(dve, 0, finish)
            dve_norm(dve, 2, w["h"])


def build_experts(nc, w, inp, out):
    ctx = ExitStack()
    with ctx:
        def sb(name, shape, dt=FP32):
            return ctx.enter_context(nc.sbuf_tensor(name, shape, dt))

        def sem(name):
            return ctx.enter_context(nc.semaphore(name))

        at = Attention(nc, ctx, w, causal=False)
        h, yy = w["h"], sb("yy", [128, T2C])
        wa = [sb(f"wa_{i}", [128, 128]) for i in range(4)]
        w1 = [sb(f"w1_{r}", [128, HID]) for r in range(2)]
        w2 = [sb(f"w2_{r}", [128, 2, 128]) for r in range(2)]
        b1, b2 = sb("b1", [128, 2]), sb("b2", [128, 1])
        zh = [[sb(f"zh_{r}{m}", [128, HALF]) for m in range(2)] for r in range(2)]
        row, top, idx = sb("row", [1, 32]), sb("top", [1, 8]), sb("idx", [1, 8], U32)
        nxt, nxt_i = sb("nxt", [1, 1]), sb("nxt_i", [1, 1], I32)
        word = sb("word", [1, 4], I32)

        zeroed, att_loaded, hid_loaded, ffn_loaded = sem("ex_zeroed"), sem("att_loaded"), sem("hid_loaded"), sem("ffn_loaded")
        row_full, pick, word_done, word_read = sem("row_full"), sem("pick"), sem("word_done"), sem("word_read")
        wo_full, h_att, z1_full, zh_act, zh_dve, z2_full, h_ffn = (
            sem("wo_full"), sem("h_att"), sem("z1_full"), sem("zh_act"), sem("zh_dve"), sem("z2_full"), sem("h_ffn"))
        added, stored, passed = sem("added"), sem("stored"), sem("passed")
        NCH, GRP = T2C // HALF, Attention.GRP
        ATT_LOADS, HID_LOADS, FFN_LOADS = 8 * 16, 3 * 16, 4 * 16
        RUNS = (4, 3, 3)
        PICK = 9

        def col(c):
            return slice(c * HALF, (c + 1) * HALF)

        def run(eng, attend, feed, select=None, end=None):
            word_regs = [eng.alloc_register(f"word{i}") for i in range(4)]
            n_steps, n_att, n_ffn = (eng.alloc_register(name) for name in ("n_steps", "n_att", "n_ffn"))
            for reg, first in ((n_steps, 0), (n_att, 1), (n_ffn, 1)):
                eng.reg_mov(reg, first)
            eng.wait_ge(word_done, 1)
            eng.reg_load(word_regs, word[0:1, 0:4]).then_inc(word_read, 1)

            def end_if_past():
                if end:
                    with eng.If(eng.snap(word_regs[0]) > NSTEP - 1):
                        end(eng.snap(n_att), eng.snap(n_ffn))

            end_if_past()

            def step():
                with eng.If(eng.snap(word_regs[0]) < NSTEP):
                    b = eng.snap(word_regs[0], min_val=0, max_val=NSTEP - 1)
                    e = b * NOPS + eng.snap(word_regs[3], min_val=0, max_val=NOPS - 1)
                    with eng.If(eng.snap(word_regs[1]) > 0):
                        attend(eng.snap(n_att), eng.snap(n_ffn), e)
                        eng.reg_add(n_att, n_att, 1)
                    with eng.If(eng.snap(word_regs[2]) > 0):
                        feed(eng.snap(n_ffn), eng.snap(n_att), e, eng.snap(n_steps) + 1, b)
                        eng.reg_add(n_ffn, n_ffn, 1)
                    if select:
                        with eng.If(eng.snap(word_regs[2]) == 0):
                            select(eng.snap(n_steps) + 1, eng.snap(n_att), b)
                    settle(eng, word_done, eng.snap(n_steps) + 2, passed)
                    eng.reg_add(n_steps, n_steps, 1)
                    eng.reg_load(word_regs, word[0:1, 0:4]).then_inc(word_read, 1)
                    end_if_past()

            with eng.Fori(0, RUNS[0]):
                with eng.If(eng.snap(word_regs[0]) < NSTEP):
                    with eng.Fori(0, RUNS[1]):
                        with eng.If(eng.snap(word_regs[0]) < NSTEP):
                            with eng.Fori(0, RUNS[2]):
                                step()

        block = ctx.enter_context(nc.Block())

        @block.sync
        def _(sp):
            def attend(k, kf, e):
                settle(sp, h_att, NCH * k, passed)
                for i, name in enumerate(("wq", "wk", "wv", "wo")):
                    src = inp[name].rearrange("b o i j -> i (b o) j")[:, bass.ds(e, 1), :].rearrange("i a j -> i (a j)")
                    for r in range(2):
                        s = slice(C * r, C * r + C)
                        sp.dma_start(wa[i][s, s], src).then_inc(att_loaded, 16)

            def feed(k, ka, e, j, b):
                settle(sp, h_ffn, NCH * k, passed)
                s1 = inp["ffn_w1"].rearrange("b o i j -> i (b o) j")[:, bass.ds(e, 1), :].rearrange("i a j -> i (a j)")
                for r in range(2):
                    sp.dma_start(w1[r][C * r:C * r + C, :], s1).then_inc(hid_loaded, 16)
                sb1 = inp["ffn_b1"].rearrange("b o (m i) -> i m (b o)", m=2)[:, :, bass.ds(e, 1)]
                sp.dma_start(b1[:, :].unsqueeze(2), sb1, allow_slow_non_contiguous=True).then_inc(hid_loaded, 16)
                s2 = inp["ffn_w2"].rearrange("b o (m i) j -> i (b o) m j", m=2)[:, bass.ds(e, 1), :, :].rearrange("i a m j -> i (a m) j")
                for r in range(2):
                    sp.dma_start(w2[r][:, :, C * r:C * r + C], s2).then_inc(ffn_loaded, 16)
                sb2 = inp["ffn_b2"].rearrange("b o i -> i (b o)")[:, bass.ds(e, 1)]
                for r in range(2):
                    sp.dma_start(b2[C * r:C * r + C, :], sb2).then_inc(ffn_loaded, 16)

            for loaded, count in ((att_loaded, ATT_LOADS), (hid_loaded, HID_LOADS), (ffn_loaded, FFN_LOADS)):
                sp.sem_inc(loaded, count)
            sp.wait_ge(zeroed, 8)
            run(sp, attend, feed)
            dst = out.rearrange("(p r) c h w -> r c p (h w)", r=2)
            for p in range(2):
                sp.wait_ge(added, 2 * p + 2)
                for r in range(2):
                    sp.dma_start(dst[r, :, p, :], yy[C * r:C * r + C, p * L:(p + 1) * L]).then_inc(stored, 16)
            sp.wait_ge(stored, 4 * 16)

        @block.gpsimd
        def _(pool):
            for t in wa:
                nc.gpsimd.memset(t[:, :], 0.0).then_inc(zeroed, 1)
            for t in w1:
                nc.gpsimd.memset(t[:, :], 0.0).then_inc(zeroed, 1)
            for t in w2:
                nc.gpsimd.memset(t[:, :, :], 0.0).then_inc(zeroed, 1)
            at.prepare_pool(pool)
            at.prime_pool(pool)
            pool.wait_ge(at.at_zero, 3)
            run(pool, lambda k, kf, e: at.pool_all(pool, k), lambda k, ka, e, j, b: None)

        @block.tensor
        def _(pe):
            def attend(k, kf, e):
                pe.wait_ge(att_loaded, ATT_LOADS * k + ATT_LOADS)
                pe.wait_ge(h_ffn, NCH * kf)
                at.pe_project(pe, k, h, lambda eng, c: None, wa[0], wa[1], wa[2])
                at.pe_all(pe, k)
                for c in range(NCH):
                    pe.wait_ge(at.ot_out, GRP * k + 4 * c + 4)
                    if c >= 2:
                        pe.wait_ge(h_att, NCH * k + c - 1)
                    nc.tensor.matmul(at.pt[c % 2][:, :], wa[3][:, :], yy[:, col(c)], start=True, stop=True).then_inc(wo_full, 1)

            def hidden(k, c):
                for r in range(2):
                    for m, used in ((0, zh_act), (1, zh_dve)):
                        if c:
                            pe.wait_ge(used, 2 * (NCH * k + c - 1) + r + 1)
                        nc.tensor.matmul(at.s[r][:, col(m)], w1[r][:, 128 * m:128 * m + 128], h[:, col(c)],
                                         start=True, stop=True).then_inc(z1_full, 1)

            def feed(k, ka, e, j, b):
                pe.wait_ge(hid_loaded, HID_LOADS * k + HID_LOADS)
                pe.wait_ge(h_ffn, NCH * k)
                pe.wait_ge(h_att, NCH * ka)
                hidden(k, 0)
                for c in range(NCH):
                    if c + 1 < NCH:
                        hidden(k, c + 1)
                    if c == 0:
                        pe.wait_ge(ffn_loaded, FFN_LOADS * k + FFN_LOADS)
                    pe.wait_ge(zh_act, 2 * (NCH * k + c) + 2)
                    pe.wait_ge(zh_dve, 2 * (NCH * k + c) + 2)
                    if c >= 2:
                        pe.wait_ge(h_ffn, NCH * k + c - 1)
                    for n, (r, m) in enumerate(((0, 0), (0, 1), (1, 0), (1, 1))):
                        last = nc.tensor.matmul(at.pt[c % 2][:, :], w2[r][:, m, :], zh[r][m][:, :],
                                                start=(n == 0), stop=(n == 3))
                    last.then_inc(z2_full, 1)
                    if c == 1:
                        pe.wait_ge(h_ffn, NCH * k + 1)
                        turn_row()

            def turn_row():
                nc.tensor.transpose(at.ob[0][:, 0:128], h[:, 0:128], w["cst"][:, IDN:IDN + 128]).then_inc(row_full, 1)

            def select(j, ka, b):
                pe.wait_ge(h_att, NCH * ka)
                turn_row()

            turn_row()
            at.prime_pe(pe)
            at.prime(pe, (wo_full, NCH), (z1_full, 4 * NCH), (z2_full, NCH))
            run(pe, attend, feed, select)

        @block.scalar
        def _(act):
            def attend(k, kf, e):
                at.act_project(act, k)
                at.act_all(act, k)

            def feed(k, ka, e, j, b):
                for c in range(NCH):
                    for r in range(2):
                        act.wait_ge(z1_full, 4 * (NCH * k + c) + 2 * r + 1)
                        if r == 0:
                            act.wait_ge(z2_full, NCH * k + c)
                        nc.scalar.activation(zh[r][0][:, :], at.s[r][:, col(0)], ACT.Relu, bias=b1[:, 0:1]).then_inc(zh_act, 1)

            at.prime_act(act)
            at.prime(act, (zh_act, 2 * NCH))
            run(act, attend, feed)

        @block.vector
        def _(dve):
            def finish(eng, k, g):
                n = GRP * k + g
                eng.wait_ge(at.ot_full, n + 1)
                nc.vector.tensor_scalar(yy[:, bass.ds(g * 128, 128)], at.ob[1][:, 256:384], 1.0, None, ALU.mult).then_inc(at.ot_out, 1)

            def attend(k, kf, e):
                at.dve_project(dve, k)
                at.dve_all(dve, k, finish)
                for c in range(NCH):
                    dve.wait_ge(wo_full, NCH * k + c + 1)
                    nc.vector.tensor_copy(h[:, col(c)], at.pt[c % 2][:, :]).then_inc(h_att, 1)

            def feed(k, ka, e, j, b):
                for c in range(NCH):
                    for r in range(2):
                        dve.wait_ge(z1_full, 4 * (NCH * k + c) + 2 * r + 2)
                        if r == 0:
                            dve.wait_ge(z2_full, NCH * k + c)
                        nc.vector.tensor_scalar(zh[r][1][:, :], at.s[r][:, col(1)], b1[:, 1:2], 0.0, ALU.add, ALU.max).then_inc(zh_dve, 1)
                    if c == 2:
                        write_word(j, b)
                    dve.wait_ge(z2_full, NCH * k + c + 1)
                    nc.vector.tensor_scalar(h[:, col(c)], at.pt[c % 2][:, :], b2[:, :], None, ALU.add).then_inc(h_ffn, 1)
                    if c == 1:
                        argmax(j)

            def argmax(j):
                base = PICK * j
                dve.wait_ge(row_full, j + 1)
                nc.vector.tensor_copy(row[:, 0:NOPS], at.ob[0][0:1, 0:NOPS]).then_inc(pick, 1)
                settle(dve, pick, base + 1, passed)
                nc.vector.max(top[:, :], row[:, 0:NOPS]).then_inc(pick, 1)
                settle(dve, pick, base + 2, passed)
                nc.vector.max_index(idx[:, :], top[:, :], row[:, 0:NOPS]).then_inc(pick, 1)

            def write_word(j, b):
                base = PICK * j
                settle(dve, pick, base + 3, passed)
                op = dve.value_load(idx[0:1, 0:1], min_val=0, max_val=NOPS - 1)
                at_step = (b + 1) * NOPS + op
                nc.vector.tensor_reduce(nxt[:, :], w["code"][0:1, bass.DynSlice(at_step, NSTEP, NOPS)], AX.X, ALU.min).then_inc(pick, 1)
                dve.wait_ge(pick, base + 4)
                nc.vector.tensor_copy(nxt_i[:, :], nxt[:, :]).then_inc(pick, 1)
                dve.wait_ge(pick, base + 5)
                atleast(dve, word_read, 5 * j)
                nc.vector.tensor_scalar(word[:, 0:1], nxt_i[:, :], 2, None, ALU.arith_shift_right).then_inc(pick, 1)
                nc.vector.tensor_scalar(word[:, 1:2], nxt_i[:, :], 1, None, ALU.bitwise_and).then_inc(pick, 1)
                nc.vector.tensor_scalar(word[:, 2:3], nxt_i[:, :], 1, 1, ALU.arith_shift_right, ALU.bitwise_and).then_inc(pick, 1)
                nc.vector.tensor_copy(word[:, 3:4], idx[:, 0:1]).then_inc(pick, 1)
                dve.wait_ge(pick, base + PICK)
                dve.sem_inc(word_done, 1)

            def select(j, ka, b):
                argmax(j)
                write_word(j, b)

            def end(ka, kf):
                settle(dve, h_att, NCH * ka, passed)
                settle(dve, h_ffn, NCH * kf, passed)
                for c in range(NCH):
                    nc.vector.tensor_tensor(yy[:, col(c)], w["t2"][:, col(c)], h[:, col(c)], ALU.add).then_inc(added, 1)

            at.prime_dve(dve)
            at.prime(dve, (h_att, NCH), (h_ffn, NCH), (zh_dve, 2 * NCH))
            select(0, 0, -1)
            run(dve, attend, feed, select, end)


INPUTS = {"x": "x", "gamma": "L0_conv_gamma", "beta": "L0_conv_beta", "W_in": "L0_conv_W_in",
          "conv_w": "L0_conv_conv_w", "conv_b": "L0_conv_conv_b", "W_x": "L0_conv_W_x", "W_dt": "L0_conv_W_dt",
          "b_dt": "L0_conv_b_dt", "A_log": "L0_conv_A_log", "D_skip": "L0_conv_D_skip", "W_out": "L0_conv_W_out",
          "W_p": "L0_conv_W_p", "b_p": "L0_conv_b_p", "s1": "L0_conv_s1", "s2": "L0_conv_s2",
          "Wq": "L1_attn_Wq", "Wk": "L1_attn_Wk", "Wv": "L1_attn_Wv",
          "ffn_w1": "L1_ffn_ffn_w1", "ffn_b1": "L1_ffn_ffn_b1", "ffn_w2": "L1_ffn_ffn_w2", "ffn_b2": "L1_ffn_ffn_b2",
          "wq": "L1_ffn_wq", "wk": "L1_ffn_wk", "wv": "L1_ffn_wv", "wo": "L1_ffn_wo",
          "attn_mask": "L1_ffn_attn_mask", "ffn_mask": "L1_ffn_ffn_mask"}


def program(nc, inp, out):
    ctx = ExitStack()
    with ctx:
        shapes = {"cst": [128, CONSTW], "xst": [128, T2C], "gam": [128, 1], "bet": [128, 1], "bp": [128, 1],
                  "eps": [128, 1], "wp": [128, 128], "wq1": [128, 128], "wk1": [128, 128], "wv1": [128, 128],
                  "xm2": [128, T2C], "code": [1, 2 * NSTEP * NOPS + NOPS]}
        scan_only = {"xs": [128, NSEQ * XW], "cb": [128, 1], "hcb": [128, 1], "bdt": [128, 1], "dsk": [128, 1],
                     "scol": [128, 2], "aneg": [128, NS], "wca": [128, 128], "wcb": [128, 128], "wg": [128, 128],
                     "wbc": [128, 128], "wdt": [128, 128], "wo": [128, 128]}
        w = {name: ctx.enter_context(nc.sbuf_tensor("w_" + name, shape, FP32)) for name, shape in shapes.items()}
        with ExitStack() as scans:
            for name, shape in scan_only.items():
                w[name] = scans.enter_context(nc.sbuf_tensor("w_" + name, shape, FP32))
            w["sel"] = scans.enter_context(nc.sbuf_tensor("w_sel", [128, 32, 128], BF16))
            build_prepare(nc, w, inp)
            with nc.sbuf_tensor("w_xm", [128, B * L], FP32) as w["xm"]:
                build_scan(nc, w, inp)
        w["t2"] = ctx.enter_context(nc.sbuf_tensor("w_t2", [128, T2C], FP32))
        w["h"] = ctx.enter_context(nc.sbuf_tensor("w_h", [128, T2C], FP32))
        build_attend(nc, w, inp)
        build_experts(nc, w, inp, out)


def constants():
    import numpy as np

    t = np.zeros((128, CONSTW), np.float32)
    r = np.arange(128)
    t[:, IDN:IDN + 128] = np.eye(128)
    chan = np.concatenate([np.arange(C), C + (np.arange(C) % 8) * 8 + np.arange(C) // 8])
    t[:, PAIR:PAIR + 128] = 0.5 * (chan[:, None] // 2 == chan[None, :] // 2)
    same = (r[:, None] // C == r[None, :] // C)
    t[:, MEAN:MEAN + 128] = same / C
    t[:, CEN:CEN + 128] = np.eye(128) - same / C
    t[:, CAUS:CAUS + 128] = np.where(r[None, :] <= r[:, None], 0.0, -1e30)
    for part in (0, 64, 96):
        t[part:part + 32, SELV:SELV + 32] = np.eye(32)
    t[:, IOTA:IOTA + 72] = 4 * np.arange(72)
    return t


def kernel(**inputs):
    import numpy as np
    import concourse.bacc as bacc
    from concourse.bass_utils import run_bass_kernel_spmd

    nc = bacc.Bacc("TRN2", target_bir_lowering=False, num_devices=1)
    arrays, inp = {}, {}
    for name, given in INPUTS.items():
        a = np.ascontiguousarray(inputs[given])
        if a.dtype == np.bool_:
            a = np.concatenate([a.reshape(-1), np.zeros(4 * MASKW - a.size, np.bool_)]).view(np.int32)
        arrays["in_" + name] = a
    arrays["in_consts"] = constants()
    for name, a in arrays.items():
        inp[name[3:]] = nc.dram_tensor(name, a.shape, mybir.dt.from_np(a.dtype), kind="ExternalInput").ap()
    out = nc.dram_tensor("out", (B, C, 32, 32), FP32, kind="ExternalOutput").ap()
    program(nc, inp, out)
    r = run_bass_kernel_spmd(nc, [arrays], core_ids=[0])
    return r.results[0]["out"]
```
